# Optimizing a Trainium2 kernel written in Bass

```python
import numpy as np
import jax
import jax.numpy as jnp

def _softmax(x, axis=-1):
    return jax.nn.softmax(x, axis=axis)

def _gelu(x):
    return jax.nn.gelu(x, approximate=True)

def _silu(x):
    return jax.nn.silu(x)

def _sigmoid(x):
    return jax.nn.sigmoid(x)

def _layernorm(x, axis=-1, eps=1e-05):
    m = jnp.mean(x, axis=axis, keepdims=True)
    v = jnp.var(x, axis=axis, keepdims=True)
    return (x - m) / jnp.sqrt(v + eps)

def _scatter_add(tgt, idx, src, axis=0):
    return tgt.at[idx].add(src)

def _segment_sum(src, seg, n):
    return jax.ops.segment_sum(src, seg, n)
kernel_name = 'mk_vit_tower_d1_tok_img1024_r4_29ede4'

def setup_inputs(seed: int=0):
    np.random.seed(seed)
    _w = jnp.asarray

    def _rec_inputs():
        import jax
        import jax.numpy as jnp
        _rk = jax.random.key(seed)
        x = jax.random.uniform(jax.random.fold_in(_rk, 1), (32, 3, 256, 256), jnp.float32, 0.0, 1)
        return x
    x = _rec_inputs()

    def _L0_tok_setup():
        import jax, jax.numpy as jnp
        import numpy as np
        _GRAY_W = (0.2989, 0.587, 0.114)
        key = jax.random.key(seed)
        x = jax.random.uniform(key, (32, 3, 256, 256), dtype=jnp.float32)
        sx = jnp.array([[-3.0, 0.0, 3.0], [-10.0, 0.0, 10.0], [-3.0, 0.0, 3.0]], dtype=jnp.float32)
        scharr = jnp.stack([sx, sx.T])[:, None, :, :]
        return {'x': x, 'scharr': scharr}
    _L0_tok_all = _L0_tok_setup()
    _L0_tok_in = {k: v for k, v in _L0_tok_all.items() if k in ('scharr',)}
    del _L0_tok_all

    def _L0_attn_setup():
        import jax, jax.numpy as jnp
        import numpy as np
        B, N, DIM = (4, 256, 256)
        H, DH = (16, 64)
        NUM_MEM = 4
        TOPK = 64
        QK_SCALE = 10.0

        def l2norm(t, eps=1e-12):
            return t / jnp.clip(jnp.linalg.norm(t, axis=-1, keepdims=True), eps)
        key = jax.random.key(seed)
        ks = jax.random.split(key, 12)
        s = 0.02
        inp = {'x': jax.random.normal(ks[0], (B, N, DIM), dtype=jnp.float32), 'Wq': jax.random.normal(ks[1], (DIM, H * DH), dtype=jnp.float32) * s, 'Wk': jax.random.normal(ks[2], (DIM, H * DH), dtype=jnp.float32) * s, 'Wv': jax.random.normal(ks[3], (DIM, H * DH), dtype=jnp.float32) * s, 'W_pre_th': jax.random.normal(ks[4], (H, H), dtype=jnp.float32) * (1.0 / H) ** 0.5, 'W_post_th': jax.random.normal(ks[5], (H, H), dtype=jnp.float32) * (1.0 / H) ** 0.5, 'mem_k': jax.random.normal(ks[6], (H, NUM_MEM, DH), dtype=jnp.float32), 'mem_v': jax.random.normal(ks[7], (H, NUM_MEM, DH), dtype=jnp.float32), 'head_scale_params': jnp.ones((1, H, 1, 1), dtype=jnp.float32), 'Wg': jax.random.normal(ks[8], (DIM, H * DH), dtype=jnp.float32) * s, 'bg': jnp.ones((H * DH,), dtype=jnp.float32), 'Wo': jax.random.normal(ks[9], (H * DH, DIM), dtype=jnp.float32) * s}
        return inp
    _L0_attn_all = _L0_attn_setup()
    _L0_attn_in = {k: v for k, v in _L0_attn_all.items() if k in ('Wq', 'Wk', 'Wv', 'W_pre_th', 'W_post_th', 'mem_k', 'mem_v', 'head_scale_params', 'Wg', 'bg', 'Wo')}
    del _L0_attn_all

    def _L0_ffn_setup():
        import jax, jax.numpy as jnp
        import numpy as np
        B, S, D = (4, 512, 256)
        N_EXPERTS, EXPERT_SIZE = (16, 64)
        WIDTH = N_EXPERTS * EXPERT_SIZE
        key = jax.random.key(seed)
        k_x, k_w1, k_w2, k_g = jax.random.split(key, 4)
        x = jax.random.normal(k_x, (B, S, D), dtype=jnp.float32)
        w1 = jax.random.normal(k_w1, (D, WIDTH), dtype=jnp.float32) / np.sqrt(D).astype(np.float32)
        b1 = jnp.zeros((WIDTH,), dtype=jnp.float32)
        w2 = jax.random.normal(k_w2, (WIDTH, D), dtype=jnp.float32) / np.sqrt(WIDTH).astype(np.float32)
        b2 = jnp.zeros((D,), dtype=jnp.float32)
        return {'x': x, 'w1': w1, 'b1': b1, 'w2': w2, 'b2': b2}
    _L0_ffn_all = _L0_ffn_setup()
    _L0_ffn_in = {k: v for k, v in _L0_ffn_all.items() if k in ('w1', 'b1', 'w2', 'b2')}
    del _L0_ffn_all
    return {'x': x, 'L0_tok_scharr': _L0_tok_in['scharr'], 'L0_attn_Wq': _L0_attn_in['Wq'], 'L0_attn_Wk': _L0_attn_in['Wk'], 'L0_attn_Wv': _L0_attn_in['Wv'], 'L0_attn_W_pre_th': _L0_attn_in['W_pre_th'], 'L0_attn_W_post_th': _L0_attn_in['W_post_th'], 'L0_attn_mem_k': _L0_attn_in['mem_k'], 'L0_attn_mem_v': _L0_attn_in['mem_v'], 'L0_attn_head_scale_params': _L0_attn_in['head_scale_params'], 'L0_attn_Wg': _L0_attn_in['Wg'], 'L0_attn_bg': _L0_attn_in['bg'], 'L0_attn_Wo': _L0_attn_in['Wo'], 'L0_ffn_w1': _L0_ffn_in['w1'], 'L0_ffn_b1': _L0_ffn_in['b1'], 'L0_ffn_w2': _L0_ffn_in['w2'], 'L0_ffn_b2': _L0_ffn_in['b2']}

def reference(x, L0_tok_scharr, L0_attn_Wq, L0_attn_Wk, L0_attn_Wv, L0_attn_W_pre_th, L0_attn_W_post_th, L0_attn_mem_k, L0_attn_mem_v, L0_attn_head_scale_params, L0_attn_Wg, L0_attn_bg, L0_attn_Wo, L0_ffn_w1, L0_ffn_b1, L0_ffn_w2, L0_ffn_b2):
    import jax
    import jax.numpy as jnp

    def _L0_tok_ref(x, scharr):
        import jax, jax.numpy as jnp
        import numpy as np
        _GRAY_W = (0.2989, 0.587, 0.114)
        w = jnp.asarray(_GRAY_W, dtype=x.dtype)
        gray = jnp.einsum('bchw,c->bhw', x, w)[:, None]
        edges = jax.lax.conv_general_dilated(gray, scharr, window_strides=(1, 1), padding='SAME', dimension_numbers=('NCHW', 'OIHW', 'NCHW'))
        abs_edges = jnp.sqrt(jnp.square(edges))
        edge = abs_edges.sum(axis=1) / 2
        return edge

    def _L0_attn_ref(x, Wq, Wk, Wv, W_pre_th, W_post_th, mem_k, mem_v, head_scale_params, Wg, bg, Wo):
        import jax, jax.numpy as jnp
        import numpy as np
        B, N, DIM = (4, 256, 256)
        H, DH = (16, 64)
        NUM_MEM = 4
        TOPK = 64
        QK_SCALE = 10.0

        def l2norm(t, eps=1e-12):
            return t / jnp.clip(jnp.linalg.norm(t, axis=-1, keepdims=True), eps)
        b, n, _ = x.shape
        q = (x @ Wq).reshape(b, n, H, DH).transpose(0, 2, 1, 3)
        k = (x @ Wk).reshape(b, n, H, DH).transpose(0, 2, 1, 3)
        v = (x @ Wv).reshape(b, n, H, DH).transpose(0, 2, 1, 3)
        mk = jnp.broadcast_to(mem_k[None], (b, H, NUM_MEM, DH))
        mv = jnp.broadcast_to(mem_v[None], (b, H, NUM_MEM, DH))
        k = jnp.concatenate([mk, k], axis=2)
        v = jnp.concatenate([mv, v], axis=2)
        q = l2norm(q)
        k = l2norm(k)
        dots = jnp.einsum('bhid,bhjd->bhij', q, k) * QK_SCALE
        dots = jnp.einsum('hg,bgij->bhij', W_pre_th, dots)
        mask_value = -jnp.finfo(dots.dtype).max
        j = n + NUM_MEM
        col_pos = jnp.arange(j) - NUM_MEM
        causal = jnp.arange(n)[:, None] < col_pos[None, :]
        dots = jnp.where(causal[None, None], mask_value, dots)
        top = jax.lax.top_k(dots, TOPK)[0]
        vk = top[..., -1:]
        dots = jnp.where(dots < vk, mask_value, dots)
        attn = jax.nn.softmax(dots, axis=-1)
        attn = jnp.einsum('hg,bgij->bhij', W_post_th, attn)
        out = jnp.einsum('bhij,bhjd->bhid', attn, v)
        out = out * head_scale_params
        out = out.transpose(0, 2, 1, 3).reshape(b, n, H * DH)
        gates = x @ Wg + bg
        out = out * jax.nn.sigmoid(gates)
        return out @ Wo

    def _L0_ffn_ref(x, w1, b1, w2, b2):
        import jax, jax.numpy as jnp
        import numpy as np
        B, S, D = (4, 512, 256)
        N_EXPERTS, EXPERT_SIZE = (16, 64)
        WIDTH = N_EXPERTS * EXPERT_SIZE
        h = jax.nn.relu(jnp.einsum('bsd,dw->bsw', x, w1) + b1)
        return jnp.einsum('bsw,wd->bsd', h, w2) + b2
    h = _L0_tok_ref(x, L0_tok_scharr)
    h = h + _L0_attn_ref(_layernorm(h, axis=-1), L0_attn_Wq, L0_attn_Wk, L0_attn_Wv, L0_attn_W_pre_th, L0_attn_W_post_th, L0_attn_mem_k, L0_attn_mem_v, L0_attn_head_scale_params, L0_attn_Wg, L0_attn_bg, L0_attn_Wo)
    h = h + _L0_ffn_ref(_layernorm(h, axis=-1), L0_ffn_w1, L0_ffn_b1, L0_ffn_w2, L0_ffn_b2)
    return h

_drawn_inputs = setup_inputs


def setup_inputs(seed=0):
    import zlib

    import numpy as np

    out = dict(_drawn_inputs(seed))
    spreads = {'L0_attn_head_scale_params': (1.0, 0.6),
     'L0_attn_bg': (1.0, 0.6),
     'L0_ffn_b1': (0.0, 0.324),
     'L0_ffn_b2': (0.0, 0.1)}
    factors = {'L0_attn_Wk': 3.85, 'L0_attn_W_pre_th': 2.764, 'L0_attn_mem_k': 3.49, 'L0_attn_Wg': 8.0}
    for name, (base, spread) in spreads.items():
        noise = np.random.default_rng([zlib.crc32(name.encode()), seed]).standard_normal(out[name].shape)
        drawn = base * np.exp(spread * noise) if base else spread * noise
        out[name] = jnp.asarray(drawn.astype(out[name].dtype))
    for name, factor in factors.items():
        out[name] = (out[name] * factor).astype(out[name].dtype)
    return out
```

```python
from contextlib import ExitStack

import concourse.bass as bass
from concourse import mybir

F32 = mybir.dt.float32
ALU = mybir.AluOpType
ACT = mybir.ActivationFunctionType

P = 128
GRAY = (0.2989, 0.587, 0.114)
LN_EPS = 1e-5
NORM_EPS = 1e-12
QK_SCALE = 10.0
TOPK = 64
MASKED = -1e30
TAKEN = -3e38

SCHEDULE = {
    0: (("next", "load_x"), ("cur", "dots1a"), ("prev", "values1")),
    1: (("cur", "dots1b"),),
    2: (("prev", "project1"),),
    3: (("prev", "norm2"), ("cur", "v"), ("cur", "keep_h")),
    4: (("cur", "gate"), ("next", "gray")),
    5: (("prev", "xn2_t"), ("next", "halo")),
    6: (("next", "edges"), ("prev", "ffn_up")),
    7: (("next", "norm1"), ("prev", "ffn_down")),
    8: (("next", "xn_t"), ("next", "q")),
    9: (("next", "sum_q"), ("cur", "values0"), ("next", "k")),
    10: (("next", "sum_k"), ("cur", "project0")),
    11: (("next", "scale_k"),),
    12: (("next", "dots0"),),
}


class Tally:

    def __init__(self, eng):
        self.eng, self.seen = eng, {}

    def __call__(self, sem, events=1):
        self.seen[sem.name] = (sem, self.seen.get(sem.name, (sem, 0))[1] + events)
        return self.seen[sem.name][1]

    def peek(self, sem, events=1):
        return self.seen.get(sem.name, (sem, 0))[1] + events

    def settle(self):
        for sem, events in self.seen.values():
            self.eng.sem_inc(sem, -events)
        self.seen = {}


def vit_layer(nc, x, scharr, Wq, Wk, Wv, W_pre, W_post, mem_k, mem_v, head_scale, Wg, bg, Wo, w1, b1, w2, b2, out):
    B, C, N, D = x.shape
    H, MEM, DH = mem_k.shape
    HD = H * DH
    KT = D // P
    TT = N // P
    FT = HD // P
    WF = w1.shape[1] // P
    J = MEM + N
    R = P // H
    NB = N // R
    NP = NB // 2
    J0 = MEM + P
    I1 = P - R
    REST = J - 2 * P
    assert H * R == P and TT == 2 and KT == 2 and 2 * DH == P and WF == FT == 8 and 0 < REST <= R

    def cols(b):
        return MEM + R * (b + 1)

    def plan(b):
        n = cols(b)
        if n <= TOPK:
            return "all", 0, 0
        drop = n - TOPK
        low = drop // 8 + 1
        return ("low", low, drop % 8) if low < 8 else ("top", TOPK // 8, 7)

    with ExitStack() as ctx:
        def sb(name, shape):
            return ctx.enter_context(nc.sbuf_tensor(name, shape, F32))

        def sem(name):
            return ctx.enter_context(nc.semaphore(name))

        wq_sb, wk_sb, wv_sb, wg_sb = (sb(f"w{c}_sb", [P, KT, HD]) for c in "qkvg")
        w1_sb = sb("w1_sb", [P, KT, WF * P])
        w2_sb = sb("w2_sb", [P, WF, D])
        wo_sb = sb("wo_sb", [P, FT, D])
        half_bg = sb("half_bg", [P, FT])
        b1_sb = sb("b1_sb", [P, WF])
        b2_sb = sb("b2_sb", [P, D])
        ident = sb("ident", [P, P])
        bands = sb("bands", [P, 2, 3, P])
        pre_mix = sb("pre_mix", [P, P])
        post_mix = sb("post_mix", [P, P])
        future = sb("future", [P, R])
        head_sel = sb("head_sel", [P, 2])
        power = sb("power", [P, 64])
        x_in = sb("x_in", [P, C, TT, D])
        gray = sb("gray", [P, TT, D + 2])
        edge_hi = sb("edge_hi", [P, HD])
        edge_lo = sb("edge_lo", [P, 2, TT, P])
        h_new = sb("h_new", [P, TT, D])
        h_cur = sb("h_cur", [P, TT, D])
        h_mid = sb("h_mid", [P, TT, D])
        xn = sb("xn", [P, TT, D])
        xn_t = sb("xn_t", [P, KT, J])
        xn2_t = sb("xn2_t", [P, KT, N])
        out_sb = sb("out_sb", [P, TT, D])
        q_t = sb("q_t", [P, FT, N])
        k_t = sb("k_t", [P, FT, J])
        v_sb = sb("v_sb", [P, 2, HD])
        gate_t = sb("gate_t", [P, FT, N])
        wide = sb("wide", [P, FT, N])
        dots0 = sb("dots0", [P, H, J0])
        dots1 = sb("dots1", [P, H, J])
        by_row = sb("by_row", [P, 2, 2, J])
        scores = sb("scores", [P, 4, 2, J])
        probs = sb("probs", [P, 2, 2, J])
        work = sb("work", [P, 2, J])
        negated = sb("negated", [P, 2, J])
        mix_n = sb("mix_n", [P, 2, 2, P])
        pt0 = sb("pt0", [P, H, N])
        pt1 = sb("pt1", [P, H, N - I1])
        heads_t = sb("heads_t", [P, FT, P])
        stats = sb("stats", [P, TT, 6])
        mv = sb("mv", [P, TT, 2])
        rstd = sb("rstd", [P, TT])
        shift = sb("shift", [P, TT])
        sumsq = sb("sumsq", [P, 2, TT, H])
        rnorm = sb("rnorm", [P, 2, TT, H])
        qscale = sb("qscale", [P, TT, H])
        top8 = sb("top8", [P, 2, 8])
        cut8 = sb("cut8", [P, 2, 8])
        neg_max = sb("neg_max", [P, 2, 2])
        total = sb("total", [P, 2, 2])
        inv_total = sb("inv_total", [P, 2, 2])

        halo = edge_hi[32:35, 0:TT * D].rearrange("p (t d) -> p t d", t=TT)
        halo_w = edge_lo[32:35]
        rk_wide = wide[:].rearrange("p f n -> p (f n)")
        v_rest = edge_hi[0:REST, :]
        pt_rest = edge_lo[0:REST].rearrange("p a b c -> p (a b c)")[:, 0:H * R].rearrange("p (h r) -> p h r", h=H)

        banks = [ctx.enter_context(nc.psum_tensor(f"bank{i}", [P, 512], F32)) for i in range(4)]
        score_ps = [ctx.enter_context(nc.psum_tensor(f"score_ps{i}", [P, 512], F32)) for i in range(2)]
        pt_ps = [ctx.enter_context(nc.psum_tensor(f"pt_ps{i}", [P, 512], F32)) for i in range(2)]

        loaded_pool = sem("loaded_pool")
        loaded_pe = sem("loaded_pe")
        zeroed = sem("zeroed")
        gray_halo = sem("gray_halo")
        const_pe = sem("const_pe")
        const_act = sem("const_act")
        const_dve = sem("const_dve")
        pool_step = sem("pool_step")
        act_step = sem("act_step")
        dve_step = sem("dve_step")
        block_step = [sem(f"block_step{k}") for k in range(2)]
        pe_act = [sem(f"bank{i}_full_for_act") for i in range(4)]
        pe_dve = [sem(f"bank{i}_full_for_dve") for i in range(4)]
        bank_free = [sem(f"bank{i}_free") for i in range(4)]
        x_here = sem("x_here")
        x_used = sem("x_used")
        gray_ready = sem("gray_ready")
        halo_here = sem("halo_here")
        abs_ready = sem("abs_ready")
        h_ready = sem("h_ready")
        h_mid_ready = sem("h_mid_ready")
        mv_ready = sem("mv_ready")
        rstd_ready = sem("rstd_ready")
        xn_ready = sem("xn_ready")
        qk_copied = sem("qk_copied")
        squares_ready = sem("squares_ready")
        squares_used = sem("squares_used")
        sumsq_ready = sem("sumsq_ready")
        rk_ready = sem("rk_ready")
        rq_ready = sem("rq_ready")
        dots_ready = sem("dots_ready")
        mem_v_here = sem("mem_v_here")
        gates_ready = sem("gates_ready")
        xn2_done = sem("xn2_done")
        hidden_used = sem("hidden_used")
        h_cur_ready = sem("h_cur_ready")
        out_ready = sem("out_ready")
        out_stored = sem("out_stored")
        by_row_here = [sem(f"by_row_here{i}") for i in range(2)]
        by_row_free = [sem(f"by_row_free{i}") for i in range(2)]
        score_full = [sem(f"score_full{k}") for k in range(2)]
        score_free = [sem(f"score_free{k}") for k in range(2)]
        scores_ready = sem("scores_ready")
        scores_free = sem("scores_free")
        max_ready = sem("max_ready")
        exp_ready = sem("exp_ready")
        inv_ready = sem("inv_ready")
        mix_ready = sem("mix_ready")
        pt_full = [sem(f"pt_full{k}") for k in range(2)]
        pt_free = [sem(f"pt_free{k}") for k in range(2)]

        block = ctx.enter_context(nc.Block())

        UNITS = ([f"dots1.{h}" for h in range(8)] + ["values1.0", "values1.1"] + [f"dots1.{h}" for h in range(8, 16)]
                 + ["project1"] + [f"v.{i}" for i in range(6)] + [f"gate.{i}" for i in range(4)] + ["xn2_t"]
                 + ["edges.0", "edges.1"] + [f"ffn_up.{i}" for i in range(4)] + ["ffn_down", "xn_t"]
                 + [f"q.{i}" for i in range(4)] + ["sum_q", "values0.0", "values0.1"] + [f"k.{i}" for i in range(4)]
                 + ["sum_k", "project0"] + [f"scale_k.{i}" for i in range(4)] + [f"dots0.{i}" for i in range(8)])
        BANK = {u: i % 4 for i, u in enumerate(UNITS)}

        def bank(u):
            return banks[BANK[u]]

        def run(core, background, prologue, epilogue, settle, eng):
            def batch(first, last, i):
                for s in range(NP):
                    core(s, last)
                    for whose, step in SCHEDULE.get(s, ()):
                        if not (whose == "prev" and first or whose == "next" and last):
                            background(step, i)
                settle()

            prologue()
            for s in range(NP):
                for whose, step in SCHEDULE.get(s, ()):
                    if whose == "next":
                        background(step, -1)
            core(None, False)
            settle()
            batch(True, False, 0)
            with eng.Fori(1, B - 1) as i:
                batch(False, False, i)
            batch(False, True, B - 1)
            for s in range(NP):
                for whose, step in SCHEDULE.get(s, ()):
                    if whose == "prev":
                        background(step, B)
            epilogue()
            settle()

        @block.sync
        def _(sp):
            tally = Tally(sp)

            def prologue():
                for r in range(2):
                    sp.sem_inc(by_row_free[r], 2)
                sp.wait_ge(zeroed, tally(zeroed))
                with nc.allow_non_contiguous_dma(reason="weights of a few hundred words, once"):
                    for r in range(R):
                        for w, t in ((W_pre, pre_mix), (W_post, post_mix)):
                            sp.dma_start(t[H * r:H * r + H, H * r:H * r + H],
                                           w.rearrange("h g -> g h")).then_inc(loaded_pool, 16)
                    for k in range(2):
                        for t, dy, col in ((0, 2, P - 1), (1, 0, 0)):
                            sp.dma_start(halo_w[:, k, t, col:col + 1],
                                           scharr[k, 0, dy:dy + 1, :].rearrange("a b -> b a")).then_inc(loaded_pool, 16)
                    sp.dma_start(dots1[:, 3, 0:18],
                                   scharr.rearrange("a b c d -> (a b c d)").partition_broadcast(P)).then_inc(loaded_pool, 16)
                    sp.dma_start(b2_sb[:], b2.partition_broadcast(P)).then_inc(loaded_pool, 16)
                    sp.dma_start(b1_sb[:], b1.rearrange("(f p) -> p f", p=P)).then_inc(loaded_pool, 16)
                    sp.dma_start(half_bg[:], bg.rearrange("(f p) -> p f", p=P)).then_inc(loaded_pool, 16)
                    for e in range(2):
                        sp.dma_start(dots1[DH * e:DH * e + DH, 4, 0:FT],
                                       head_scale.rearrange("a (f e) b c -> (a b c) e f", e=2)[0, e].partition_broadcast(DH)
                                       ).then_inc(loaded_pool, 16)
                    sp.dma_start(wo_sb[:], Wo.rearrange("(f p) n -> p f n", p=P)).then_inc(loaded_pool, 16)
                    for e in range(2):
                        sp.dma_start(dots1[0:H * MEM, 5 + e, 0:DH],
                                       mem_k.rearrange("h m d -> (h m) d")).then_inc(loaded_pool, 16)
                for dst, src in ((wq_sb, Wq), (wk_sb, Wk), (wv_sb, Wv), (wg_sb, Wg), (w1_sb, w1)):
                    sp.dma_start(dst[:], src.rearrange("(k p) n -> p k n", p=P)).then_inc(loaded_pe, 16)
                sp.dma_start(w2_sb[:], w2.rearrange("(k p) n -> p k n", p=P)).then_inc(loaded_pe, 16)

            def regroup(p):
                r = p % 2
                sp.wait_ge(by_row_free[r], tally(by_row_free[r], 2))
                for k in range(2):
                    b = 2 * p + k
                    src = dots0 if b < NB // 2 else dots1
                    i0 = R * (b % (NB // 2))
                    sp.dma_start(by_row[:, r, k, 0:cols(b)], src[i0:i0 + R, :, 0:cols(b)]).then_inc(by_row_here[r], 16)

            def core(s, last):
                pass

            def background(step, i):
                if step == "dots1a":
                    sp.wait_ge(dots_ready, tally(dots_ready))
                    for p in range(NP // 2, NP):
                        regroup(p)
                if step == "ffn_down":
                    sp.wait_ge(out_ready, tally(out_ready))
                    sp.dma_start(out[i - 1].rearrange("(t p) d -> p t d", p=P), out_sb[:]).then_inc(out_stored, 16)
                if step == "dots0":
                    sp.wait_ge(dots_ready, tally(dots_ready))
                    for p in range(NP // 2):
                        regroup(p)

            run(core, background, prologue, lambda: None, tally.settle, sp)

        @block.gpsimd
        def _(pool):
            tally = Tally(pool)

            def chain(ins):
                ins.then_inc(pool_step, 1)
                pool.wait_ge(pool_step, tally(pool_step))

            def prologue():
                for t in (ident, pre_mix, post_mix, future, head_sel, pt0, pt1, edge_lo, xn_t, gray):
                    chain(pool.memset(t[:], 0.0))
                chain(pool.memset(power[:], -0.5))
                chain(pool.memset(head_sel[0:DH, 0:1], 1.0))
                chain(pool.memset(head_sel[DH:P, 1:2], 1.0))
                chain(pool.affine_select(out=ident[:], in_=ident[:], compare_op=ALU.not_equal, fill=1.0,
                                         base=0, pattern=[[-1, P]], channel_multiplier=1))
                chain(pool.affine_select(out=future[:], in_=future[:], compare_op=ALU.is_ge, fill=MASKED,
                                         base=0, pattern=[[-H, R]], channel_multiplier=1))
                taps = dots1[:, 0:3, 0:P]
                chain(pool.memset(taps, 0.0))
                for dy in range(3):
                    chain(pool.affine_select(out=dots1[:, dy, 0:P], in_=dots1[:, dy, 0:P], compare_op=ALU.not_equal,
                                             fill=1.0, base=1 - dy, pattern=[[-1, P]], channel_multiplier=1))
                pool.sem_inc(zeroed, 1)
                pool.wait_ge(loaded_pool, tally(loaded_pool, 16 * (2 * R + 4 + 4 + 2 + 1 + 2)))
                chain(pool.tensor_scalar(half_bg[:], half_bg[:], 0.5, 1.0, ALU.mult, ALU.mult))
                for k in range(2):
                    for dx in range(3):
                        for dy in range(3):
                            tap = dots1[:, 3, 9 * k + 3 * dy + dx:9 * k + 3 * dy + dx + 1]
                            if dy == 0:
                                chain(pool.tensor_scalar(bands[:, k, dx, :], dots1[:, dy, 0:P], tap, 1.0, ALU.mult, ALU.mult))
                            else:
                                chain(pool.tensor_scalar(dots1[:, 7, 0:P], dots1[:, dy, 0:P], tap, 1.0, ALU.mult, ALU.mult))
                                chain(pool.tensor_tensor(bands[:, k, dx, :], bands[:, k, dx, :], dots1[:, 7, 0:P], ALU.add))
                for f in range(FT):
                    chain(pool.tensor_scalar(wo_sb[:, f, :], wo_sb[:, f, :], dots1[:, 4, f:f + 1], 0.5, ALU.mult, ALU.mult))
                pool.sem_inc(const_dve, 1)
                pool.wait_ge(mv_ready, tally(mv_ready))
                mem = slice(0, H * MEM)
                chain(pool.tensor_scalar(total[mem, 0, 0:1], total[mem, 0, 0:1], NORM_EPS * NORM_EPS, 1.0, ALU.max, ALU.mult))
                chain(pool.tensor_tensor(total[mem, 0, 1:2], total[mem, 0, 0:1], power[mem, 0:1], ALU.pow))
                for e in range(2):
                    chain(pool.tensor_scalar(dots0[mem, 0, DH * e:DH * e + DH], dots1[mem, 5 + e, 0:DH], total[mem, 0, 1:2], 1.0,
                                             ALU.mult, ALU.mult))
                pool.sem_inc(const_pe, 1)
                pool.sem_inc(const_act, 1)

            def normalise_prepare():
                pool.wait_ge(mv_ready, tally(mv_ready, 2))
                chain(pool.tensor_scalar(rstd[:], mv[:, :, 1], LN_EPS, 1.0, ALU.add, ALU.mult))
                chain(pool.tensor_tensor(rstd[:], rstd[:], power[:, 0:TT], ALU.pow))
                chain(pool.tensor_tensor(shift[:], mv[:, :, 0], rstd[:], ALU.mult))
                chain(pool.tensor_scalar(shift[:], shift[:], -1.0, 1.0, ALU.mult, ALU.mult))
                pool.sem_inc(rstd_ready, 1)

            def square(src, first_wait):
                pool.wait_ge(qk_copied, tally(qk_copied))
                if first_wait is not None:
                    pool.wait_ge(first_wait, tally(first_wait))
                for u in range(FT // 2):
                    pool.tensor_tensor(wide[:, 2 * u:2 * u + 2, :], src[:, 2 * u:2 * u + 2], src[:, 2 * u:2 * u + 2],
                                       ALU.mult).then_inc(squares_ready, 1)

            def core(s, last):
                if s is None:
                    return
                pool.wait_ge(inv_ready, tally(inv_ready))
                for k in range(2):
                    pool.tensor_scalar(mix_n[:, s % 2, k, :], post_mix[:], inv_total[:, s % 2, k:k + 1], 1.0,
                                       ALU.mult, ALU.mult).then_inc(mix_ready, 1)

            def background(step, i):
                if step == "norm2":
                    normalise_prepare()
                if step == "keep_h":
                    chain(pool.tensor_copy(h_cur[:], h_new[:]))
                    pool.sem_inc(h_cur_ready, 1)
                if step == "gray":
                    pool.wait_ge(x_here, tally(x_here, 16))
                    inner = gray[:, :, 1:D + 1]
                    chain(pool.tensor_scalar(inner, x_in[:, 0], GRAY[0], 1.0, ALU.mult, ALU.mult))
                    for c in (1, 2):
                        chain(pool.tensor_scalar(x_in[:, c], x_in[:, c], GRAY[c], 1.0, ALU.mult, ALU.mult))
                        chain(pool.tensor_tensor(inner, inner, x_in[:, c], ALU.add))
                    pool.sem_inc(gray_ready, 1)
                    pool.sem_inc(x_used, 1)
                    pool.sem_inc(gray_halo, 1)
                if step == "xn2_t":
                    pool.wait_ge(xn2_done, tally(xn2_done))
                    for t in range(TT):
                        chain(pool.tensor_tensor(h_mid[:, t], h_mid[:, t], b2_sb[:], ALU.add))
                    pool.sem_inc(h_mid_ready, 1)
                if step == "edges":
                    pool.wait_ge(abs_ready, tally(abs_ready))
                    chain(pool.tensor_tensor(h_new[:], h_new[:], xn[:], ALU.add))
                    pool.sem_inc(h_ready, 1)
                if step == "norm1":
                    normalise_prepare()
                if step == "q":
                    square(q_t, hidden_used)
                if step == "k":
                    square(k_t[:, :, MEM:J], squares_used)
                if step == "sum_k":
                    pool.wait_ge(sumsq_ready, tally(sumsq_ready))
                    chain(pool.tensor_scalar(sumsq[:], sumsq[:], NORM_EPS * NORM_EPS, 1.0, ALU.max, ALU.mult))
                    chain(pool.tensor_tensor(rnorm[:].rearrange("p a b c -> p (a b c)"),
                                             sumsq[:].rearrange("p a b c -> p (a b c)"), power[:], ALU.pow))
                    chain(pool.tensor_copy(rk_wide.rearrange("p (a d) -> p a d", d=DH),
                                           rnorm[:, 1].rearrange("p t h -> p (t h)").unsqueeze(2).to_broadcast([P, TT * H, DH])))
                    pool.sem_inc(rk_ready, 1)
                    chain(pool.tensor_scalar(qscale[:], rnorm[:, 0], QK_SCALE, 1.0, ALU.mult, ALU.mult))
                    pool.sem_inc(rq_ready, 1)

            run(core, background, prologue, lambda: None, tally.settle, pool)

        @block.tensor
        def _(pe):
            tally = Tally(pe)

            def take_bank(u):
                pe.wait_ge(bank_free[BANK[u]], tally(bank_free[BANK[u]]))
                return bank(u)

            def copied(u):
                pe.wait_ge(bank_free[BANK[u]], tally.peek(bank_free[BANK[u]]))

            def prologue():
                for k in range(2):
                    pe.sem_inc(score_free[k], 1)
                    pe.sem_inc(pt_free[k], 1)
                for i in range(4):
                    pe.sem_inc(bank_free[i], 1)
                pe.wait_ge(const_pe, tally(const_pe))
                pe.wait_ge(loaded_pe, tally(loaded_pe, 16 * 6))
                ps = take_bank("scale_k.0")
                pe.transpose(ps[:, 0:H * MEM], dots0[0:H * MEM, 0, 0:P], ident[0:H * MEM, 0:H * MEM]
                             ).then_inc(pe_act[BANK["scale_k.0"]], 1)

            def score_products(p):
                r = p % 2
                pe.wait_ge(by_row_here[r], tally(by_row_here[r], 32))
                for k in range(2):
                    n = cols(2 * p + k)
                    pe.wait_ge(score_free[k], tally(score_free[k]))
                    pe.matmul(score_ps[k][:, 0:n], pre_mix[:], by_row[:, r, k, 0:n], start=True, stop=False
                              ).then_inc(by_row_free[r], 1)
                    pe.matmul(score_ps[k][:, n - R:n], ident[:], future[:], start=False, stop=True,
                              ).then_inc(score_full[k], 1)

            def core(s, last):
                if s is None:
                    score_products(0)
                    score_products(1)
                    return
                if s + 2 < NP or not last:
                    score_products((s + 2) % NP)
                for k in range(2):
                    b = 2 * s + k
                    n = cols(b)
                    pe.wait_ge(mix_ready, tally(mix_ready))
                    pe.wait_ge(pt_free[k], tally(pt_free[k]))
                    tiles = [(j, min(j + P, n)) for j in range(0, n, P)]
                    for t, (j0, j1) in enumerate(tiles):
                        last_mm = pe.matmul(pt_ps[k][0:j1 - j0, P * t:P * t + P], probs[:, s % 2, k, j0:j1], mix_n[:, s % 2, k, :],
                                            start=True, stop=True)
                    last_mm.then_inc(pt_full[k], 1)

            def values(t):
                i0 = P * t
                for g in range(2):
                    ps = take_bank(f"values{t}.{g}")
                    for f in range(FT // 2):
                        for e in range(2):
                            h = 2 * (FT // 2 * g + f) + e
                            o = ps[DH * e:DH * e + DH, P * f:P * f + P]
                            vs = slice(DH * h, DH * h + DH)
                            mm = pe.matmul(o, v_sb[:, 0, vs], pt0[:, h, i0:i0 + P], start=True, stop=False)
                            if t == 0:
                                mm = pe.matmul(o[:, I1:P], v_sb[:, 1, vs], pt1[:, h, 0:R], start=False, stop=True)
                            else:
                                mm = pe.matmul(o, v_sb[:, 1, vs], pt1[:, h, R:R + P], start=False, stop=False)
                                mm = pe.matmul(o[:, P - R:P], v_rest[:, vs], pt_rest[:, h, :], start=False, stop=True)
                    mm.then_inc(pe_dve[BANK[f"values{t}.{g}"]], 1)

            def project(t):
                copied(f"values{t}.0")
                copied(f"values{t}.1")
                ps = take_bank(f"project{t}")
                for f in range(FT):
                    mm = pe.matmul(ps[:, 0:D], heads_t[:, f, :], wo_sb[:, f, :], start=(f == 0), stop=(f == FT - 1))
                mm.then_inc(pe_dve[BANK[f"project{t}"]], 1)

            def features(name, w, src, units):
                for u in range(units):
                    ps = take_bank(f"{name}.{u}")
                    for e in range(2):
                        f = 2 * u + e
                        for c in range(KT):
                            mm = pe.matmul(ps[:, N * e:N * e + N], w[:, c, P * f:P * f + P], src[:, c],
                                           start=(c == 0), stop=(c == KT - 1))
                    mm.then_inc(pe_act[BANK[f"{name}.{u}"]], 1)

            def sums_of_squares(u):
                ps = take_bank(u)
                for f in range(FT):
                    if f % 2 == 0:
                        pe.wait_ge(squares_ready, tally(squares_ready))
                    for t in range(TT):
                        at = H * t + 2 * f
                        mm = pe.matmul(ps[:, at:at + 2], wide[:, f, P * t:P * t + P], head_sel[:], start=True, stop=True)
                mm.then_inc(pe_act[BANK[u]], 1)

            def transposes(u, dst_act):
                ps = take_bank(u)
                for c in range(KT):
                    for t in range(TT):
                        mm = pe.transpose(ps[:, N * c + P * t:N * c + P * t + P], xn[:, t, P * c:P * c + P], ident[:])
                mm.then_inc(dst_act[BANK[u]], 1)

            def dots(name, t, heads, n):
                ps = take_bank(name)
                for at, h in enumerate(heads):
                    rows = slice(DH * (h % 2), DH * (h % 2) + DH)
                    mm = pe.matmul(ps[:, n * at:n * at + n], q_t[rows, h // 2, P * t:P * t + P], k_t[rows, h // 2, 0:n],
                                   start=True, stop=True)
                mm.then_inc(pe_act[BANK[name]], 1)

            def background(step, i):
                if step in ("dots1a", "dots1b"):
                    for h in range(8) if step == "dots1a" else range(8, 16):
                        dots(f"dots1.{h}", 1, [h], J)
                if step == "values1":
                    for k in range(2):
                        pe.wait_ge(pt_free[k], tally.peek(pt_free[k]))
                    values(1)
                if step == "values0":
                    for k in range(2):
                        pe.wait_ge(pt_free[k], tally.peek(pt_free[k]))
                    pe.wait_ge(mem_v_here, tally(mem_v_here, 16))
                    values(0)
                if step == "project1":
                    project(1)
                if step == "project0":
                    project(0)
                if step == "v":
                    for u in range(6):
                        ps = take_bank(f"v.{u}")
                        jt, half = divmod(u, 2)
                        m = P if jt < 2 else REST
                        for c in range(KT):
                            mm = pe.matmul(ps[0:m, :], xn_t[:, c, P * jt:P * jt + m], wv_sb[:, c, 512 * half:512 * half + 512],
                                           start=(c == 0), stop=(c == KT - 1))
                        mm.then_inc(pe_act[BANK[f"v.{u}"]], 1)
                if step == "gate":
                    features("gate", wg_sb, xn_t[:, :, MEM:J], FT // 2)
                if step == "xn2_t":
                    pe.wait_ge(xn_ready, tally(xn_ready, 2))
                    transposes("xn2_t", pe_act)
                if step == "edges":
                    pe.wait_ge(gray_ready, tally(gray_ready))
                    pe.wait_ge(halo_here, tally(halo_here, 16 * 6))
                    for k in range(2):
                        ps = take_bank(f"edges.{k}")
                        for t in range(TT):
                            for dx in range(3):
                                pe.matmul(ps[:, D * t:D * t + D], bands[:, k, dx, :], gray[:, t, dx:dx + D],
                                          start=(dx == 0), stop=False)
                            mm = pe.matmul(ps[:, D * t:D * t + D], halo_w[:, k, t, :], halo[:, t, :], start=False, stop=True)
                        mm.then_inc(pe_act[BANK[f"edges.{k}"]], 1)
                if step == "ffn_up":
                    copied("xn2_t")
                    features("ffn_up", w1_sb, xn2_t, WF // 2)
                if step == "xn_t":
                    pe.wait_ge(xn_ready, tally(xn_ready, 2))
                    transposes("xn_t", pe_act)
                if step == "ffn_down":
                    for u in range(WF // 2):
                        copied(f"ffn_up.{u}")
                    ps = take_bank("ffn_down")
                    for t in range(TT):
                        for f in range(WF):
                            mm = pe.matmul(ps[:, D * t:D * t + D], wide[:, f, P * t:P * t + P], w2_sb[:, f, :],
                                           start=(f == 0), stop=(f == WF - 1))
                    mm.then_inc(pe_dve[BANK["ffn_down"]], 1)
                if step == "q":
                    copied("xn_t")
                    features("q", wq_sb, xn_t[:, :, MEM:J], FT // 2)
                if step == "k":
                    features("k", wk_sb, xn_t[:, :, MEM:J], FT // 2)
                if step in ("sum_q", "sum_k"):
                    sums_of_squares(step)
                if step == "scale_k":
                    pe.wait_ge(rk_ready, tally(rk_ready))
                    for u in range(FT // 2):
                        ps = take_bank(f"scale_k.{u}")
                        for e in range(2):
                            f = 2 * u + e
                            for t in range(TT):
                                mm = pe.matmul(ps[:, N * e + P * t:N * e + P * t + P],
                                               rk_wide[:, HD * t + P * f:HD * t + P * f + P], ident[:], start=True, stop=True)
                        mm.then_inc(pe_dve[BANK[f"scale_k.{u}"]], 1)
                if step == "dots0":
                    for u in range(FT // 2):
                        copied(f"scale_k.{u}")
                    for u in range(8):
                        h = 4 * (u // 2) + u % 2
                        dots(f"dots0.{u}", 0, [h, h + 2], J0)

            run(core, background, prologue, lambda: None, tally.settle, pe)

        @block.scalar
        def _(act):
            tally = Tally(act)

            def full(u):
                act.wait_ge(pe_act[BANK[u]], tally(pe_act[BANK[u]]))
                return bank(u)

            def both(ins, u, ready):
                ins.then_inc(act_step, 1)
                act.wait_ge(act_step, tally(act_step))
                act.sem_inc(bank_free[BANK[u]], 1)
                act.sem_inc(ready, 1)

            def free(ins, u):
                ins.then_inc(bank_free[BANK[u]], 1)

            def halves(ps):
                return ps[:].rearrange("p (e n) -> p e n", e=2)

            def prologue():
                act.sem_inc(scores_free, 4)
                act.sem_inc(x_used, 1)
                act.wait_ge(const_act, tally(const_act))
                ps = full("scale_k.0")
                for e in range(2):
                    rows = slice(DH * e, DH * e + DH)
                    src = ps[rows, 0:H * MEM].rearrange("p (f e m) -> p f e m", e=2, m=MEM)[:, :, e, :]
                    ins = act.copy(k_t[rows, :, 0:MEM], src)
                free(ins, "scale_k.0")

            def copy_scores(p):
                act.wait_ge(scores_free, tally(scores_free))
                for k in range(2):
                    n = cols(2 * p + k)
                    act.wait_ge(score_full[k], tally(score_full[k]))
                    ins = act.copy(scores[:, p % 4, k, 0:n], score_ps[k][:, 0:n])
                    if k == 0:
                        ins.then_inc(score_free[0], 1)
                ins.then_inc(act_step, 1)
                act.wait_ge(act_step, tally(act_step))
                act.sem_inc(score_free[1], 1)
                act.sem_inc(scores_ready, 1)

            def exponentials(p):
                act.wait_ge(max_ready, tally(max_ready))
                for k in range(2):
                    b = 2 * p + k
                    n = cols(b)
                    total_out = total[:, p % 2, k:k + 1] if plan(b)[0] == "all" else None
                    act.activation(probs[:, p % 2, k, 0:n], scores[:, p % 4, k, 0:n], ACT.Exp,
                                   bias=neg_max[:, p % 2, k:k + 1], accum_out=total_out).then_inc(exp_ready, 1)

            def copy_probs(s):
                for k in range(2):
                    b = 2 * s + k
                    n = cols(b)
                    act.wait_ge(pt_full[k], tally(pt_full[k]))
                    for t, j0 in enumerate(range(0, n, P)):
                        m = min(P, n - j0)
                        src = pt_ps[k][0:m, P * t:P * t + P].rearrange("p (r h) -> p h r", h=H)
                        dst = (pt0[0:m, :, R * b:R * b + R], pt1[0:m, :, R * b - I1:R * b - I1 + R] if b >= NB // 2 - 1 else None,
                               pt_rest)[t]
                        ins = act.copy(dst, src)
                    ins.then_inc(pt_free[k], 1)

            def core(s, last):
                if s is None:
                    copy_scores(0)
                    copy_scores(1)
                    exponentials(0)
                    return
                if s + 2 < NP or not last:
                    copy_scores((s + 2) % NP)
                if s + 1 < NP or not last:
                    exponentials((s + 1) % NP)
                copy_probs(s)

            def normalise(src, t_ready):
                for t in range(TT):
                    act.activation(xn[:, t], src[:, t], ACT.Identity, bias=shift[:, t:t + 1], scale=rstd[:, t:t + 1]
                                   ).then_inc(xn_ready, 1)

            def background(step, i):
                if step in ("dots1a", "dots1b"):
                    for h in range(8) if step == "dots1a" else range(8, 16):
                        u = f"dots1.{h}"
                        ps = full(u)
                        ins = act.mul(dots1[:, h, :], ps[:, 0:J], qscale[:, 1, h:h + 1])
                        both(ins, u, dots_ready) if h == H - 1 else free(ins, u)
                if step == "dots0":
                    act.wait_ge(rq_ready, tally(rq_ready))
                    for n in range(8):
                        u = f"dots0.{n}"
                        ps = full(u)
                        h = 4 * (n // 2) + n % 2
                        for e in range(2):
                            ins = act.mul(dots0[:, h + 2 * e, :], ps[:, J0 * e:J0 * e + J0], qscale[:, 0, h + 2 * e:h + 2 * e + 1])
                        both(ins, u, dots_ready) if n == 7 else free(ins, u)
                if step == "v":
                    for n in range(6):
                        u = f"v.{n}"
                        ps = full(u)
                        jt, half = divmod(n, 2)
                        m = P if jt < 2 else REST
                        dst = v_sb[:, jt] if jt < 2 else v_rest
                        ins = act.copy(dst[:, 512 * half:512 * half + 512], ps[0:m, :])
                        if n != 1:
                            free(ins, u)
                            continue
                        ins.then_inc(act_step, 1)
                        act.wait_ge(act_step, tally(act_step))
                        act.sem_inc(bank_free[BANK[u]], 1)
                        act.dma_start(v_sb[0:MEM, 0, :].rearrange("m (h d) -> m h d", h=H),
                                      mem_v.rearrange("h m d -> m h d")).then_inc(mem_v_here, 16)
                if step == "gate":
                    for n in range(FT // 2):
                        u = f"gate.{n}"
                        ps = full(u)
                        for e in range(2):
                            f = 2 * n + e
                            ins = act.activation(gate_t[:, f, :], ps[:, N * e:N * e + N], ACT.Tanh,
                                                 bias=half_bg[:, f:f + 1], scale=0.5)
                        both(ins, u, gates_ready) if n == FT // 2 - 1 else free(ins, u)
                if step == "norm2":
                    act.wait_ge(rstd_ready, tally(rstd_ready))
                    normalise(h_mid, None)
                if step == "xn2_t":
                    u = "xn2_t"
                    ps = full(u)
                    both(act.copy(xn2_t[:], halves(ps)), u, xn2_done)
                if step == "edges":
                    for k, dst in ((0, h_new), (1, xn)):
                        u = f"edges.{k}"
                        ps = full(u)
                        ins = act.activation(dst[:], halves(ps), ACT.Abs, scale=0.5)
                        both(ins, u, abs_ready) if k == 1 else free(ins, u)
                if step == "ffn_up":
                    for n in range(WF // 2):
                        u = f"ffn_up.{n}"
                        ps = full(u)
                        for e in range(2):
                            f = 2 * n + e
                            ins = act.activation(wide[:, f, :], ps[:, N * e:N * e + N], ACT.Relu, bias=b1_sb[:, f:f + 1])
                        free(ins, u)
                if step == "norm1":
                    act.wait_ge(rstd_ready, tally(rstd_ready))
                    normalise(h_new, None)
                if step == "xn_t":
                    free(act.copy(xn_t[:, :, MEM:J], halves(full("xn_t"))), "xn_t")
                if step in ("q", "k"):
                    dst = q_t if step == "q" else k_t[:, :, MEM:J]
                    for n in range(FT // 2):
                        u = f"{step}.{n}"
                        ps = full(u)
                        ins = act.copy(dst[:, 2 * n:2 * n + 2], halves(ps))
                        both(ins, u, qk_copied) if n == FT // 2 - 1 else free(ins, u)
                if step in ("sum_q", "sum_k"):
                    n = ("sum_q", "sum_k").index(step)
                    ps = full(step)
                    both(act.copy(sumsq[:, n].rearrange("p t h -> p (t h)"), ps[:, 0:TT * H]), step, (squares_used, sumsq_ready)[n])
                if step == "halo":
                    act.wait_ge(gray_halo, tally(gray_halo))
                    for dx in range(3):
                        act.dma_start(halo[dx:dx + 1, 0, :], gray[0:1, 1, dx:dx + D]).then_inc(halo_here, 16)
                        act.dma_start(halo[dx:dx + 1, 1, :], gray[P - 1:P, 0, dx:dx + D]).then_inc(halo_here, 16)
                if step == "load_x":
                    act.wait_ge(x_used, tally(x_used))
                    act.dma_start(x_in[:], x[i + 1].rearrange("c (t p) d -> p c t d", p=P)).then_inc(x_here, 16)

            run(core, background, prologue, lambda: None, tally.settle, act)

        @block.vector
        def _(dve):
            tally = Tally(dve)

            def full(u):
                dve.wait_ge(pe_dve[BANK[u]], tally(pe_dve[BANK[u]]))
                return bank(u)

            def prologue():
                dve.wait_ge(const_dve, tally(const_dve))
                mem = slice(0, H * MEM)
                dve.sem_inc(out_stored, 16)
                dve.sem_inc(hidden_used, 2)
                dve.scalar_tensor_tensor(out=dots0[mem, 1, 0:DH], in0=dots1[mem, 5, 0:DH], scalar=1.0,
                                         in1=dots1[mem, 5, 0:DH], op0=ALU.mult, op1=ALU.mult,
                                         accum_out=total[mem, 0, 0:1]).then_inc(mv_ready, 1)

            def find_cut(p):
                dve.wait_ge(scores_ready, tally(scores_ready))
                plans = [plan(2 * p + k) for k in range(2)]
                src = [scores[:, p % 4, k, 0:cols(2 * p + k)] for k in range(2)]
                wrk = [work[:, k, 0:cols(2 * p + k)] for k in range(2)]
                for k in range(2):
                    dve.max(top8[:, k, :], src[k]).then_inc(block_step[k], 1)
                for k in range(2):
                    if plans[k][0] == "low":
                        dve.tensor_scalar(negated[:, k, 0:cols(2 * p + k)], src[k], -1.0, None, ALU.mult
                                          ).then_inc(block_step[k], 1)
                        src[k] = negated[:, k, 0:cols(2 * p + k)]
                    dve.wait_ge(block_step[k], tally(block_step[k], 2 if plans[k][0] == "low" else 1))
                dve.tensor_scalar(neg_max[:, p % 2, :], top8[:, :, 0], -1.0, None, ALU.mult).then_inc(max_ready, 1)
                for k in range(2):
                    if plans[k][0] == "low":
                        dve.max(cut8[:, k, :], src[k]).then_inc(block_step[k], 1)
                for r in range(1, 8):
                    for k in range(2):
                        if r < plans[k][1]:
                            eight = top8 if r == 1 and plans[k][0] == "top" else cut8
                            if eight is cut8:
                                dve.wait_ge(block_step[k], tally(block_step[k]))
                            dve.match_replace(wrk[k], eight[:, k, :], src[k] if r == 1 else wrk[k], TAKEN
                                              ).then_inc(block_step[k], 1)
                    for k in range(2):
                        if r < plans[k][1]:
                            dve.wait_ge(block_step[k], tally(block_step[k]))
                            dve.max(cut8[:, k, :], wrk[k]).then_inc(block_step[k], 1)

            def cut_and_sum(p):
                dve.wait_ge(exp_ready, tally(exp_ready, 2))
                for k in range(2):
                    kind, rounds, at = plan(2 * p + k)
                    n = cols(2 * p + k)
                    if kind == "all":
                        continue
                    dve.wait_ge(block_step[k], tally(block_step[k]))
                    pr = probs[:, p % 2, k, 0:n]
                    dve.scalar_tensor_tensor(out=pr, in0=(scores[:, p % 4, k, 0:n] if kind == "top" else negated[:, k, 0:n]),
                                             scalar=cut8[:, k, at:at + 1], in1=pr,
                                             op0=ALU.is_ge if kind == "top" else ALU.is_le, op1=ALU.mult,
                                             accum_out=total[:, p % 2, k:k + 1]).then_inc(block_step[k], 1)
                for k in range(2):
                    if plan(2 * p + k)[0] != "all":
                        dve.wait_ge(block_step[k], tally(block_step[k]))
                dve.reciprocal(inv_total[:, p % 2, :], total[:, p % 2, :]).then_inc(inv_ready, 1)
                dve.sem_inc(scores_free, 1)

            def core(s, last):
                if s is None:
                    find_cut(0)
                    return
                cut_and_sum(s)
                if s + 1 < NP or not last:
                    find_cut((s + 1) % NP)

            def moments(src):
                for t in range(TT):
                    dve.bn_stats(stats[:, t, :], src[:, t]).then_inc(dve_step, 1)
                for t in range(TT):
                    dve.wait_ge(dve_step, tally(dve_step))
                    dve.bn_aggr(mv[:, t, :], stats[:, t, :]).then_inc(mv_ready, 1)

            def gate(t):
                for g in range(2):
                    u = f"values{t}.{g}"
                    ps = full(u)
                    fs = slice(FT // 2 * g, FT // 2 * g + FT // 2)
                    dve.scalar_tensor_tensor(out=heads_t[:, fs, :], in0=gate_t[:, fs, P * t:P * t + P], scalar=1.0,
                                             in1=ps[:].rearrange("p (f n) -> p f n", n=P), op0=ALU.add, op1=ALU.mult
                                             ).then_inc(bank_free[BANK[u]], 1)

            def add_residual(t):
                u = f"project{t}"
                ps = full(u)
                dve.tensor_tensor(h_mid[:, t], h_cur[:, t], ps[:, 0:D], ALU.add).then_inc(dve_step, 1)
                dve.wait_ge(dve_step, tally(dve_step))
                dve.sem_inc(bank_free[BANK[u]], 1)

            def background(step, i):
                if step == "values1":
                    gate(1)
                if step == "project1":
                    add_residual(1)
                    moments(h_mid)
                if step == "values0":
                    dve.wait_ge(gates_ready, tally(gates_ready))
                    gate(0)
                if step == "project0":
                    dve.wait_ge(h_cur_ready, tally(h_cur_ready))
                    add_residual(0)
                if step == "edges":
                    dve.wait_ge(h_ready, tally(h_ready))
                    moments(h_new)
                if step == "ffn_down":
                    u = "ffn_down"
                    ps = full(u)
                    dve.sem_inc(hidden_used, 1)
                    dve.wait_ge(h_mid_ready, tally(h_mid_ready))
                    dve.wait_ge(out_stored, tally(out_stored, 16))
                    dve.tensor_tensor(out_sb[:], h_mid[:], ps[:].rearrange("p (t d) -> p t d", t=TT), ALU.add
                                      ).then_inc(dve_step, 1)
                    dve.wait_ge(dve_step, tally(dve_step))
                    dve.sem_inc(bank_free[BANK[u]], 1)
                    dve.sem_inc(out_ready, 1)
                if step == "scale_k":
                    for n in range(FT // 2):
                        u = f"scale_k.{n}"
                        ps = full(u)
                        dve.tensor_tensor(k_t[:, 2 * n:2 * n + 2, MEM:J], k_t[:, 2 * n:2 * n + 2, MEM:J],
                                          ps[:].rearrange("p (e n) -> p e n", e=2), ALU.mult).then_inc(bank_free[BANK[u]], 1)

            def epilogue():
                dve.wait_ge(out_stored, tally(out_stored, 16))

            run(core, background, prologue, epilogue, tally.settle, dve)


_INS = ["x", "L0_tok_scharr", "L0_attn_Wq", "L0_attn_Wk", "L0_attn_Wv", "L0_attn_W_pre_th", "L0_attn_W_post_th", "L0_attn_mem_k",
        "L0_attn_mem_v", "L0_attn_head_scale_params", "L0_attn_Wg", "L0_attn_bg", "L0_attn_Wo", "L0_ffn_w1", "L0_ffn_b1",
        "L0_ffn_w2", "L0_ffn_b2"]


def kernel(**inputs):
    import numpy as _np
    import concourse.bacc as _bacc
    from concourse import mybir as _mybir
    from concourse.bass_utils import run_bass_kernel_spmd as _run

    nc = _bacc.Bacc("TRN2", target_bir_lowering=False, num_devices=1)
    arrays, args = {}, []
    for name in _INS:
        a = _np.ascontiguousarray(inputs[name])
        arrays[f"in_{name}_dram"] = a
        args.append(nc.dram_tensor(f"in_{name}_dram", a.shape, _mybir.dt.from_np(a.dtype), kind="ExternalInput").ap())
    n, _, rows, width = inputs["x"].shape
    out = nc.dram_tensor("out_dram", (n, rows, width), _mybir.dt.float32, kind="ExternalOutput").ap()
    vit_layer(nc, *args, out)
    r = _run(nc, [arrays], core_ids=[0])
    return r.results[0]["out_dram"]
```

```python
from contextlib import ExitStack

import concourse.bass as bass
from concourse import mybir

F32 = mybir.dt.float32
ALU = mybir.AluOpType
ACT = mybir.ActivationFunctionType

P = 128
GRAY = (0.2989, 0.587, 0.114)
LN_EPS = 1e-5
NORM_EPS = 1e-12
QK_SCALE = 10.0
TOPK = 64
MASKED = -1e30
TAKEN = -3e38

SCHEDULE = {
    0: (("cur", "softmax"), ("prev", "values", 0, 4), ("prev", "gate_heads"), ("next", "load_x"), ("prev", "move_h"), ("cur", "keep_h"),
        ("next", "gray")),
    1: (("cur", "softmax"), ("cur", "v", 0, 4),),
    2: (("cur", "softmax"), ("cur", "v", 4, 5), ("next", "edges", 0, 1)),
    3: (("cur", "softmax"), ("next", "edges", 1, 2), ("cur", "gate", 0, 1), ("next", "moments")),
    4: (("cur", "softmax"), ("cur", "gate", 1, 4), ("next", "norm1")),
    5: (("cur", "softmax"), ("prev", "project"), ("next", "xn_t")),
    6: (("cur", "softmax"), ("next", "q", 0, 3),),
    7: (("cur", "softmax"), ("prev", "norm2"), ("next", "q", 3, 4), ("next", "k", 0, 2), ("prev", "xn2_t")),
    8: (("cur", "softmax"), ("next", "k", 2, 4), ("next", "sum_q")),
    9: (("cur", "softmax"), ("next", "sum_k"), ("next", "norms_q"), ("prev", "ffn_up", 0, 1), ("next", "norms_k")),
    10: (("cur", "softmax"), ("next", "root_q", 1, 2), ("prev", "ffn_up", 1, 2)),
    11: (("cur", "softmax"), ("next", "root_q", 0, 1), ("next", "k_norms"), ("prev", "ffn_up", 2, 3), ("next", "scale_k", 0, 4),
        ("prev", "ffn_up", 3, 4)),
    12: (("cur", "softmax"), ("next", "dots1", 0, 16),),
    13: (("cur", "softmax"), ("next", "dots0", 0, 8),),
    14: (("cur", "softmax"), ("prev", "ffn_down", 0, 1),),
    15: (("cur", "softmax"), ("prev", "ffn_down", 1, 2),),
}


class Tally:

    def __init__(self, eng):
        self.eng, self.seen = eng, {}

    def __call__(self, sem, events=1):
        self.seen[sem.name] = (sem, self.seen.get(sem.name, (sem, 0))[1] + events)
        return self.seen[sem.name][1]

    def peek(self, sem, events=1):
        return self.seen.get(sem.name, (sem, 0))[1] + events

    def settle(self):
        for sem, events in self.seen.values():
            self.eng.sem_inc(sem, -events)
        self.seen = {}


def vit_layer(nc, x, scharr, Wq, Wk, Wv, W_pre, W_post, mem_k, mem_v, head_scale, Wg, bg, Wo, w1, b1, w2, b2, out):
    B, C, N, D = x.shape
    H, MEM, DH = mem_k.shape
    HD = H * DH
    KT = D // P
    TT = N // P
    FT = HD // P
    WF = w1.shape[1] // P
    J = MEM + N
    R = P // H
    NB = N // R
    NP = NB // 2
    J0 = MEM + P
    I1 = P - R
    REST = J - 2 * P
    assert H * R == P and TT == 2 and KT == 2 and 2 * DH == P and WF == FT == 8 and 0 < REST <= R

    def cols(b):
        return MEM + R * (b + 1)

    ORDER = [p for n in range(NP // 2) for p in (NP - 1 - n, n)]

    def plan(b):
        n = cols(b)
        if n <= TOPK:
            return "all", 0, 0
        drop = n - TOPK
        low = drop // 8 + 1
        return ("low", low, drop % 8) if low < 8 else ("top", TOPK // 8, 7)

    with ExitStack() as ctx:
        def sb(name, shape):
            return ctx.enter_context(nc.sbuf_tensor(name, shape, F32))

        def sem(name):
            return ctx.enter_context(nc.semaphore(name))

        wq_sb, wk_sb, wv_sb, wg_sb = (sb(f"w{c}_sb", [P, KT, HD]) for c in "qkvg")
        w1_sb = sb("w1_sb", [P, KT, WF * P])
        w2_sb = sb("w2_sb", [P, WF, D])
        wo_sb = sb("wo_sb", [P, FT, D])
        half_bg = sb("half_bg", [P, FT])
        b1_sb = sb("b1_sb", [P, WF])
        b2_sb = sb("b2_sb", [P, D])
        ident = sb("ident", [P, P])
        bands = sb("bands", [P, 2, 3, P])
        pre_mix = sb("pre_mix", [P, P])
        post_mix = sb("post_mix", [P, P])
        future = sb("future", [P, R])
        head_sel = sb("head_sel", [P, 2, 4, 32])
        head_back = sb("head_back", [P, 2, P])
        power = sb("power", [P, 1])
        x_in = sb("x_in", [P, C, TT, D])
        gray = sb("gray", [P, TT, D + 2])
        edge_hi = sb("edge_hi", [P, HD])
        edge_lo = sb("edge_lo", [P, 2, TT, P])
        h_new = sb("h_new", [P, TT, D])
        h_cur = sb("h_cur", [P, TT, D])
        h_mid = sb("h_mid", [P, TT, D])
        xn = sb("xn", [P, TT, D])
        xn_t = sb("xn_t", [P, KT, J])
        xn2_t = sb("xn2_t", [P, KT, N])
        out_sb = xn2_t
        q_t = sb("q_t", [P, FT, N])
        k_t = sb("k_t", [P, FT, J])
        v_sb = sb("v_sb", [P, 2, HD])
        gate_t = sb("gate_t", [P, FT, N])
        wide = sb("wide", [P, FT, N])
        dots0 = sb("dots0", [P, H, J0])
        dots1 = sb("dots1", [P, H, J])
        by_row = sb("by_row", [P, 2, 2, J])
        scores = sb("scores", [P, 4, 2, J])
        probs = sb("probs", [P, 2, 2, J])
        work = sb("work", [P, 2, J])
        mix_n = sb("mix_n", [P, 2, 2, P])
        pt0 = sb("pt0", [P, H, N])
        pt1 = sb("pt1", [P, H, N - I1])
        heads_t = sb("heads_t", [P, FT, N])
        stats = sb("stats", [P, TT, 6])
        mv = sb("mv", [P, 2, TT, 2])
        rstd = sb("rstd", [P, 2, TT])
        shift = sb("shift", [P, 2, TT])
        qscale = sb("qscale", [P, TT, 4, 4])
        top8 = sb("top8", [P, 2, 8])
        cut8 = sb("cut8", [P, 2, 8])
        neg_max = sb("neg_max", [P, 2, 2])
        total = sb("total", [P, 2, 2])
        inv_total = sb("inv_total", [P, 2, 2])

        halo = edge_hi[32:35, 0:TT * D].rearrange("p (t d) -> p t d", t=TT)
        halo_w = edge_lo[32:35]
        abs_v = wide[:, 0:2, :]
        squares = {"q": wide, "k": heads_t}
        sums_q, sums_k = xn[:, 0, :], xn[:, 1, :]
        norm_rows = xn[:, 0, :].rearrange("p (t n) -> p t n", t=TT)
        norm_cols = xn[:, 1, :]

        def q_scale(t, h):
            f = h // 2
            r = 2 * (f // 4) + h % 2
            return qscale[:, t, f % 4, r:r + 1]

        v_rest = edge_hi[0:REST, :]
        pt_rest = edge_lo[0:REST].rearrange("p a b c -> p (a b c)")[:, 0:H * R].rearrange("p (h r) -> p h r", h=H)

        banks = [ctx.enter_context(nc.psum_tensor(f"bank{i}", [P, 512], F32)) for i in range(4)]
        score_ps = [ctx.enter_context(nc.psum_tensor(f"score_ps{i}", [P, 512], F32)) for i in range(2)]
        pt_ps = [ctx.enter_context(nc.psum_tensor(f"pt_ps{i}", [P, 512], F32)) for i in range(2)]

        loaded_pool = sem("loaded_pool")
        loaded_pe = sem("loaded_pe")
        zeroed = sem("zeroed")
        gray_halo = sem("gray_halo")
        const_pe = sem("const_pe")
        const_act = sem("const_act")
        const_dve = sem("const_dve")
        pool_step = sem("pool_step")
        act_step = sem("act_step")
        dve_step = sem("dve_step")
        block_step = [sem(f"block_step{k}") for k in range(2)]
        pe_act = [sem(f"bank{i}_full_for_act") for i in range(4)]
        pe_dve = [sem(f"bank{i}_full_for_dve") for i in range(4)]
        bank_free = [sem(f"bank{i}_free") for i in range(4)]
        x_here = sem("x_here")
        x_used = sem("x_used")
        gray_ready = sem("gray_ready")
        halo_here = sem("halo_here")
        abs_ready = sem("abs_ready")
        h_ready = sem("h_ready")
        h_mid_ready = sem("h_mid_ready")
        mv_ready = sem("mv_ready")
        rstd_ready = sem("rstd_ready")
        xn_ready = sem("xn_ready")
        sums_ready = sem("sums_ready")
        k_root_ready = sem("k_root_ready")
        q_root_ready = sem("q_root_ready")
        dots_ready = sem("dots_ready")
        mem_v_here = sem("mem_v_here")
        gates_ready = sem("gates_ready")
        xn2_done = sem("xn2_done")
        h_kept = sem("h_kept")
        h_moved = sem("h_moved")
        h_mid_free = sem("h_mid_free")
        scores_copied = sem("scores_copied")
        out_ready = sem("out_ready")
        out_stored = sem("out_stored")
        by_row_here = [sem(f"by_row_here{i}") for i in range(2)]
        by_row_free = [sem(f"by_row_free{i}") for i in range(2)]
        score_full = [sem(f"score_full{k}") for k in range(2)]
        score_free = [sem(f"score_free{k}") for k in range(2)]
        scores_ready = sem("scores_ready")
        scores_free = sem("scores_free")
        max_ready = sem("max_ready")
        exp_ready = sem("exp_ready")
        inv_ready = sem("inv_ready")
        mix_ready = sem("mix_ready")
        pt_full = [sem(f"pt_full{k}") for k in range(2)]
        pt_free = [sem(f"pt_free{k}") for k in range(2)]

        block = ctx.enter_context(nc.Block())

        ONE_BANK = ("project", "xn_t", "xn2_t", "sum_q", "sum_k", "norms_q", "norms_k", "k_norms")
        UNITS = []
        for s in range(NP):
            for _, step, *part in SCHEDULE[s]:
                if step in ONE_BANK or step == "ffn_down" and part[0] == 0:
                    UNITS.append(step)
                elif part and step not in ("ffn_down", "root_q"):
                    UNITS.extend(f"{step}.{n}" for n in range(*part))
        BANK = {u: i % 4 for i, u in enumerate(UNITS)}

        def bank(u):
            return banks[BANK[u]]

        def run(eng, settle, prologue, background, core, after=None):
            def batch(first, last, i):
                for s in range(NP):
                    core(s, first, last)
                    for whose, step, *part in SCHEDULE[s]:
                        if not (whose == "prev" and first or whose == "next" and last):
                            background(step, i, *part)
                settle()

            prologue()
            for s in range(NP):
                for whose, step, *part in SCHEDULE[s]:
                    if whose == "next":
                        background(step, -1, *part)
            core(None, True, False)
            settle()
            batch(True, False, 0)
            with eng.Fori(1, B - 1) as i:
                batch(False, False, i)
            batch(False, True, B - 1)
            if after:
                after()
            for s in range(NP):
                for whose, step, *part in SCHEDULE[s]:
                    if whose == "prev":
                        background(step, B, *part)

        @block.sync
        def _(sp):
            tally = Tally(sp)

            def prologue():
                for r in range(2):
                    sp.sem_inc(by_row_free[r], 1)
                sp.sem_inc(x_used, 1)
                sp.wait_ge(zeroed, tally(zeroed))
                with nc.allow_non_contiguous_dma(reason="weights of a few hundred words, once"):
                    for r in range(R):
                        for w, t in ((W_pre, pre_mix), (W_post, post_mix)):
                            sp.dma_start(t[H * r:H * r + H, H * r:H * r + H],
                                           w.rearrange("h g -> g h")).then_inc(loaded_pool, 16)
                    for k in range(2):
                        for t, dy, col in ((0, 2, P - 1), (1, 0, 0)):
                            sp.dma_start(halo_w[:, k, t, col:col + 1],
                                           scharr[k, 0, dy:dy + 1, :].rearrange("a b -> b a")).then_inc(loaded_pool, 16)
                    sp.dma_start(dots1[:, 3, 0:18],
                                   scharr.rearrange("a b c d -> (a b c d)").partition_broadcast(P)).then_inc(loaded_pool, 16)
                    sp.dma_start(b2_sb[:], b2.partition_broadcast(P)).then_inc(loaded_pool, 16)
                    sp.dma_start(b1_sb[:], b1.rearrange("(f p) -> p f", p=P)).then_inc(loaded_pool, 16)
                    sp.dma_start(half_bg[:], bg.rearrange("(f p) -> p f", p=P)).then_inc(loaded_pool, 16)
                    for e in range(2):
                        sp.dma_start(dots1[DH * e:DH * e + DH, 4, 0:FT],
                                       head_scale.rearrange("a (f e) b c -> (a b c) e f", e=2)[0, e].partition_broadcast(DH)
                                       ).then_inc(loaded_pool, 16)
                    sp.dma_start(wo_sb[:], Wo.rearrange("(f p) n -> p f n", p=P)).then_inc(loaded_pool, 16)
                    for e in range(2):
                        sp.dma_start(dots1[0:H * MEM, 5 + e, 0:DH],
                                       mem_k.rearrange("h m d -> (h m) d")).then_inc(loaded_pool, 16)
                for dst, src in ((wq_sb, Wq), (wk_sb, Wk), (wv_sb, Wv), (wg_sb, Wg), (w1_sb, w1)):
                    sp.dma_start(dst[:], src.rearrange("(k p) n -> p k n", p=P)).then_inc(loaded_pe, 16)
                sp.dma_start(w2_sb[:], w2.rearrange("(k p) n -> p k n", p=P)).then_inc(loaded_pe, 16)

            def regroup(s):
                r = s % 2
                p = ORDER[s]
                if s < 2:
                    sp.wait_ge(dots_ready, tally(dots_ready))
                sp.wait_ge(by_row_free[r], tally(by_row_free[r]))
                for k in range(2):
                    b = 2 * p + k
                    src = dots0 if b < NB // 2 else dots1
                    i0 = R * (b % (NB // 2))
                    sp.dma_start(by_row[:, r, k, 0:cols(b)], src[i0:i0 + R, :, 0:cols(b)]).then_inc(by_row_here[r], 16)

            def background(step, i, lo=0, hi=1):
                if step == "load_x":
                    sp.wait_ge(x_used, tally(x_used))
                    sp.dma_start(x_in[:], x[i + 1].rearrange("c (t p) d -> p c t d", p=P)).then_inc(x_here, 16)
                if step == "gray":
                    sp.wait_ge(gray_halo, tally(gray_halo))
                    for dx in range(3):
                        sp.dma_start(halo[dx:dx + 1, 0, :], gray[0:1, 1, dx:dx + D]).then_inc(halo_here, 16)
                        sp.dma_start(halo[dx:dx + 1, 1, :], gray[P - 1:P, 0, dx:dx + D]).then_inc(halo_here, 16)
                if step == "ffn_down" and hi == 2:
                    sp.wait_ge(out_ready, tally(out_ready))
                    sp.dma_start(out[i - 1].rearrange("(t p) d -> p t d", p=P), out_sb[:]).then_inc(out_stored, 16)

            def core(s, first, last):
                if s is None:
                    for n in range(4):
                        regroup(n)
                elif s + 4 < NP or not last:
                    regroup((s + 4) % NP)

            run(sp, tally.settle, prologue, background, core)

        @block.gpsimd
        def _(pool):
            tally = Tally(pool)

            def chain(ins):
                ins.then_inc(pool_step, 1)
                pool.wait_ge(pool_step, tally(pool_step))

            def prologue():
                for t in (ident, pre_mix, post_mix, future, head_sel, pt0, pt1, edge_lo, xn_t, gray):
                    chain(pool.memset(t[:], 0.0))
                chain(pool.memset(power[:], -0.5))
                for f in range(2):
                    for e in range(2):
                        r = 2 * f + e
                        chain(pool.memset(head_sel[DH * e:DH * e + DH, f, :, r:r + 1], 1.0))
                chain(pool.affine_select(out=ident[:], in_=ident[:], compare_op=ALU.not_equal, fill=1.0,
                                         base=0, pattern=[[-1, P]], channel_multiplier=1))
                chain(pool.affine_select(out=future[:], in_=future[:], compare_op=ALU.is_ge, fill=MASKED,
                                         base=0, pattern=[[-H, R]], channel_multiplier=1))
                taps = dots1[:, 0:3, 0:P]
                chain(pool.memset(taps, 0.0))
                for dy in range(3):
                    chain(pool.affine_select(out=dots1[:, dy, 0:P], in_=dots1[:, dy, 0:P], compare_op=ALU.not_equal,
                                             fill=1.0, base=1 - dy, pattern=[[-1, P]], channel_multiplier=1))
                pool.sem_inc(zeroed, 1)
                pool.wait_ge(loaded_pool, tally(loaded_pool, 16 * (2 * R + 4 + 4 + 2 + 1 + 2)))
                chain(pool.tensor_scalar(half_bg[:], half_bg[:], 0.5, 1.0, ALU.mult, ALU.mult))
                for k in range(2):
                    for dx in range(3):
                        for dy in range(3):
                            tap = dots1[:, 3, 9 * k + 3 * dy + dx:9 * k + 3 * dy + dx + 1]
                            if dy == 0:
                                chain(pool.tensor_scalar(bands[:, k, dx, :], dots1[:, dy, 0:P], tap, 1.0, ALU.mult, ALU.mult))
                            else:
                                chain(pool.tensor_scalar(dots1[:, 7, 0:P], dots1[:, dy, 0:P], tap, 1.0, ALU.mult, ALU.mult))
                                chain(pool.tensor_tensor(bands[:, k, dx, :], bands[:, k, dx, :], dots1[:, 7, 0:P], ALU.add))
                for f in range(FT):
                    chain(pool.tensor_scalar(wo_sb[:, f, :], wo_sb[:, f, :], dots1[:, 4, f:f + 1], 0.5, ALU.mult, ALU.mult))
                pool.sem_inc(const_dve, 1)
                pool.wait_ge(mv_ready, tally(mv_ready))
                mem = slice(0, H * MEM)
                chain(pool.tensor_scalar(total[mem, 0, 0:1], total[mem, 0, 0:1], NORM_EPS * NORM_EPS, 1.0, ALU.max, ALU.mult))
                chain(pool.tensor_tensor(total[mem, 0, 1:2], total[mem, 0, 0:1], power[mem, 0:1], ALU.pow))
                for e in range(2):
                    chain(pool.tensor_scalar(dots0[mem, 0, DH * e:DH * e + DH], dots1[mem, 5 + e, 0:DH], total[mem, 0, 1:2], 1.0,
                                             ALU.mult, ALU.mult))
                pool.sem_inc(const_pe, 1)
                pool.sem_inc(const_act, 1)

            def normalise_prepare(w):
                pool.wait_ge(mv_ready, tally(mv_ready, 2))
                chain(pool.tensor_scalar(rstd[:, w], mv[:, w, :, 1], LN_EPS, 1.0, ALU.add, ALU.mult))
                chain(pool.tensor_tensor(rstd[:, w], rstd[:, w], power[:].to_broadcast([P, TT]), ALU.pow))
                chain(pool.tensor_tensor(shift[:, w], mv[:, w, :, 0], rstd[:, w], ALU.mult))
                chain(pool.tensor_scalar(shift[:, w], shift[:, w], -1.0, 1.0, ALU.mult, ALU.mult))
                pool.sem_inc(rstd_ready, 1)

            def inverse_root(norms):
                chain(pool.tensor_scalar(norms, norms, NORM_EPS * NORM_EPS, 1.0, ALU.max, ALU.mult))
                chain(pool.tensor_tensor(norms, norms, power[:].unsqueeze(2).to_broadcast([P, 4, 4]), ALU.pow))

            def mask_future(s):
                pool.wait_ge(scores_copied, tally(scores_copied))
                for k in range(2):
                    n = cols(2 * ORDER[s] + k)
                    own = scores[:, s % 4, k, n - R:n]
                    pool.tensor_tensor(own, own, future[:], ALU.add).then_inc(scores_ready, 1)

            def core(s, first, last):
                if s is None:
                    mask_future(0)
                    mask_future(1)
                elif s + 2 < NP or not last:
                    mask_future((s + 2) % NP)

            def background(step, i, lo=0, hi=1):
                if step == "norm2":
                    normalise_prepare(1)
                if step == "move_h":
                    pool.wait_ge(h_mid_free, tally(h_mid_free))
                    chain(pool.tensor_copy(h_mid[:], h_cur[:]))
                    pool.sem_inc(h_moved, 1)
                if step == "keep_h":
                    chain(pool.tensor_copy(h_cur[:], h_new[:]))
                    pool.sem_inc(h_kept, 1)
                if step == "gray":
                    pool.wait_ge(x_here, tally(x_here, 16))
                    inner = gray[:, :, 1:D + 1]
                    chain(pool.tensor_scalar(inner, x_in[:, 0], GRAY[0], 1.0, ALU.mult, ALU.mult))
                    for c in (1, 2):
                        chain(pool.tensor_scalar(x_in[:, c], x_in[:, c], GRAY[c], 1.0, ALU.mult, ALU.mult))
                        chain(pool.tensor_tensor(inner, inner, x_in[:, c], ALU.add))
                    pool.sem_inc(gray_ready, 1)
                    pool.sem_inc(x_used, 1)
                    pool.sem_inc(gray_halo, 1)
                if step == "xn2_t":
                    pool.wait_ge(xn2_done, tally(xn2_done))
                    for t in range(TT):
                        chain(pool.tensor_tensor(h_mid[:, t], h_mid[:, t], b2_sb[:], ALU.add))
                    pool.sem_inc(h_mid_ready, 1)
                if step == "edges" and hi == 2:
                    pool.wait_ge(abs_ready, tally(abs_ready))
                    chain(pool.tensor_tensor(h_new[:], h_new[:], abs_v, ALU.add))
                    pool.sem_inc(h_ready, 1)
                if step == "norm1":
                    normalise_prepare(0)
                if step == "norms_k":
                    pool.wait_ge(sums_ready, tally(sums_ready, 2))
                    for t in range(TT):
                        inverse_root(norm_rows[:, t, :].rearrange("p (g r) -> p g r", g=4)[:, :, 0:4])
                    pool.sem_inc(k_root_ready, 1)
                if step == "root_q":
                    inverse_root(qscale[:, lo])
                    chain(pool.tensor_scalar(qscale[:, lo], qscale[:, lo], QK_SCALE, 1.0, ALU.mult, ALU.mult))
                    pool.sem_inc(q_root_ready, 1)

            run(pool, tally.settle, prologue, background, core)

        @block.tensor
        def _(pe):
            tally = Tally(pe)

            holder = {}

            def take_bank(u):
                holder[BANK[u]] = u
                pe.wait_ge(bank_free[BANK[u]], tally(bank_free[BANK[u]]))
                return bank(u)

            def copied(u):
                if holder[BANK[u]] == u:
                    pe.wait_ge(bank_free[BANK[u]], tally.peek(bank_free[BANK[u]]))

            def prologue():
                for k in range(2):
                    pe.sem_inc(score_free[k], 1)
                    pe.sem_inc(pt_free[k], 1)
                for i in range(4):
                    pe.sem_inc(bank_free[i], 1)
                pe.wait_ge(const_pe, tally(const_pe))
                pe.wait_ge(loaded_pe, tally(loaded_pe, 16 * 6))
                ps = take_bank("scale_k.0")
                pe.transpose(ps[:, 0:H * MEM], dots0[0:H * MEM, 0, 0:P], ident[0:H * MEM, 0:H * MEM]
                             ).then_inc(pe_act[BANK["scale_k.0"]], 1)
                ps = take_bank("scale_k.1")
                for f in range(2):
                    mm = pe.transpose(ps[:, P * f:P * f + P], head_sel[:, f].rearrange("p g r -> p (g r)"), ident[:])
                mm.then_inc(pe_act[BANK["scale_k.1"]], 1)

            def score_products(s):
                r = s % 2
                p = ORDER[s]
                pe.wait_ge(by_row_here[r], tally(by_row_here[r], 32))
                for k in range(2):
                    n = cols(2 * p + k)
                    pe.wait_ge(score_free[k], tally(score_free[k]))
                    pe.matmul(score_ps[k][:, 0:n], pre_mix[:], by_row[:, r, k, 0:n], start=True, stop=True
                              ).then_inc(score_full[k], 1)

            def post_products(s):
                for k in range(2):
                    b = 2 * ORDER[s] + k
                    n = cols(b)
                    pe.wait_ge(mix_ready, tally(mix_ready))
                    pe.wait_ge(pt_free[k], tally(pt_free[k]))
                    tiles = [(j, min(j + P, n)) for j in range(0, n, P)]
                    for t, (j0, j1) in enumerate(tiles):
                        last_mm = pe.matmul(pt_ps[k][0:j1 - j0, P * t:P * t + P], probs[:, s % 2, k, j0:j1], mix_n[:, s % 2, k, :],
                                            start=True, stop=True)
                    last_mm.then_inc(pt_full[k], 1)

            def core(s, first, last):
                if s is None:
                    score_products(0)
                    score_products(1)
                    return
                if not (s == 0 and first):
                    post_products((s - 1) % NP)
                if s + 2 < NP or not last:
                    score_products((s + 2) % NP)

            def values():
                for k in range(2):
                    pe.wait_ge(pt_free[k], tally.peek(pt_free[k]))
                pe.wait_ge(mem_v_here, tally(mem_v_here, 16))
                for g in range(FT // 2):
                    u = f"values.{g}"
                    ps = take_bank(u)
                    for f in (2 * g, 2 * g + 1):
                        for n, (vals, pt, i0) in enumerate(((v_sb[:, 0], pt0, 0), (v_sb[:, 1], pt1, I1), (v_rest, pt_rest, N - R))):
                            for e in range(2):
                                h = 2 * f + e
                                o = ps[DH * e:DH * e + DH, N * (f % 2) + i0:N * (f % 2) + N]
                                mm = pe.matmul(o, vals[:, DH * h:DH * h + DH], pt[:, h, :], start=(n == 0), stop=(n == 2))
                    mm.then_inc(pe_dve[BANK[u]], 1)

            def project():
                for g in range(FT // 2):
                    copied(f"values.{g}")
                ps = take_bank("project")
                for t in range(TT):
                    for f in range(FT):
                        mm = pe.matmul(ps[:, D * t:D * t + D], heads_t[:, f, P * t:P * t + P], wo_sb[:, f, :],
                                       start=(f == 0), stop=(f == FT - 1))
                mm.then_inc(pe_dve[BANK["project"]], 1)

            def features(name, w, src, lo, hi):
                for u in range(lo, hi):
                    ps = take_bank(f"{name}.{u}")
                    for e in range(2):
                        f = 2 * u + e
                        for c in range(KT):
                            mm = pe.matmul(ps[:, N * e:N * e + N], w[:, c, P * f:P * f + P], src[:, c],
                                           start=(c == 0), stop=(c == KT - 1))
                    mm.then_inc(pe_act[BANK[f"{name}.{u}"]], 1)

            def sums_of_squares(u):
                for n in range(FT // 2):
                    copied(f"{u[-1]}.{n}")
                ps = take_bank(u)
                for f in range(FT):
                    g = 32 * (f % 4)
                    mm = pe.matmul(ps[g:g + 32, 0:N], head_sel[:, f // 4, 0, :], squares[u[-1]][:, f, :],
                                   start=(f < 4), stop=(f >= 4))
                mm.then_inc(pe_act[BANK[u]], 1)

            def transposes(u, dst_act):
                ps = take_bank(u)
                for c in range(KT):
                    for t in range(TT):
                        mm = pe.transpose(ps[:, N * c + P * t:N * c + P * t + P], xn[:, t, P * c:P * c + P], ident[:])
                mm.then_inc(dst_act[BANK[u]], 1)

            def dots(name, t, heads, n):
                ps = take_bank(name)
                for at, h in enumerate(heads):
                    rows = slice(DH * (h % 2), DH * (h % 2) + DH)
                    mm = pe.matmul(ps[:, n * at:n * at + n], q_t[rows, h // 2, P * t:P * t + P], k_t[rows, h // 2, 0:n],
                                   start=True, stop=True)
                mm.then_inc(pe_act[BANK[name]], 1)

            def background(step, i, lo=0, hi=1):
                if step == "dots1":
                    for u in range(FT // 2):
                        copied(f"scale_k.{u}")
                    for h in range(H):
                        dots(f"dots1.{h}", 1, [h], J)
                if step == "values":
                    values()
                if step == "project":
                    project()
                if step == "v":
                    for u in range(lo, min(hi, 4)):
                        ps = take_bank(f"v.{u}")
                        jt, half = divmod(u, 2)
                        for c in range(KT):
                            mm = pe.matmul(ps[:], xn_t[:, c, P * jt:P * jt + P], wv_sb[:, c, 512 * half:512 * half + 512],
                                           start=(c == 0), stop=(c == KT - 1))
                        mm.then_inc(pe_act[BANK[f"v.{u}"]], 1)
                    if hi == 5:
                        ps = take_bank("v.4")
                        for c in range(KT):
                            for half in range(2):
                                mm = pe.matmul(ps[32 * half:32 * half + REST, :], xn_t[:, c, 2 * P:J],
                                               wv_sb[:, c, 512 * half:512 * half + 512], start=(c == 0), stop=(c == KT - 1))
                        mm.then_inc(pe_act[BANK["v.4"]], 1)
                if step == "gate":
                    features("gate", wg_sb, xn_t[:, :, MEM:J], lo, hi)
                if step == "xn2_t":
                    pe.wait_ge(xn_ready, tally(xn_ready, 2))
                    transposes("xn2_t", pe_act)
                if step == "edges":
                    if lo == 0:
                        pe.wait_ge(gray_ready, tally(gray_ready))
                        pe.wait_ge(halo_here, tally(halo_here, 16 * 6))
                    for k in range(lo, hi):
                        ps = take_bank(f"edges.{k}")
                        for t in range(TT):
                            for dx in range(3):
                                pe.matmul(ps[:, D * t:D * t + D], bands[:, k, dx, :], gray[:, t, dx:dx + D],
                                          start=(dx == 0), stop=False)
                            mm = pe.matmul(ps[:, D * t:D * t + D], halo_w[:, k, t, :], halo[:, t, :], start=False, stop=True)
                        mm.then_inc(pe_act[BANK[f"edges.{k}"]], 1)
                if step == "ffn_up":
                    if lo == 0:
                        copied("xn2_t")
                    features("ffn_up", w1_sb, xn2_t, lo, hi)
                if step == "xn_t":
                    pe.wait_ge(xn_ready, tally(xn_ready, 2))
                    transposes("xn_t", pe_act)
                if step == "ffn_down":
                    if lo == 0:
                        for u in range(WF // 2):
                            copied(f"ffn_up.{u}")
                        take_bank("ffn_down")
                    ps = bank("ffn_down")
                    for t in range(lo, hi):
                        for f in range(WF):
                            mm = pe.matmul(ps[:, D * t:D * t + D], wide[:, f, P * t:P * t + P], w2_sb[:, f, :],
                                           start=(f == 0), stop=(f == WF - 1))
                    if hi == TT:
                        mm.then_inc(pe_dve[BANK["ffn_down"]], 1)
                if step == "q":
                    if lo == 0:
                        copied("xn_t")
                    features("q", wq_sb, xn_t[:, :, MEM:J], lo, hi)
                if step == "k":
                    features("k", wk_sb, xn_t[:, :, MEM:J], lo, hi)
                if step in ("sum_q", "sum_k"):
                    sums_of_squares(step)
                if step in ("norms_q", "norms_k"):
                    src, name = (sums_q, "sum_q") if step == "norms_q" else (sums_k, "sum_k")
                    copied(name)
                    ps = take_bank(step)
                    for t in range(TT):
                        mm = pe.transpose(ps[:, P * t:P * t + P], src[:, P * t:P * t + P], ident[:])
                    mm.then_inc(pe_act[BANK[step]], 1)
                if step == "k_norms":
                    pe.wait_ge(k_root_ready, tally(k_root_ready))
                    ps = take_bank("k_norms")
                    for t in range(TT):
                        mm = pe.transpose(ps[:, P * t:P * t + P], norm_rows[:, t, :], ident[:])
                    mm.then_inc(pe_act[BANK["k_norms"]], 1)
                if step == "scale_k":
                    copied("k_norms")
                    for g in range(4):
                        ps = take_bank(f"scale_k.{g}")
                        rows = slice(32 * g, 32 * g + 32)
                        for e in range(2):
                            mm = pe.matmul(ps[:, N * e:N * e + N], head_back[rows, e, :], norm_cols[rows], start=True, stop=True)
                        mm.then_inc(pe_dve[BANK[f"scale_k.{g}"]], 1)
                if step == "dots0":
                    for u in range(8):
                        h = 4 * (u // 2) + u % 2
                        dots(f"dots0.{u}", 0, [h, h + 2], J0)

            run(pe, tally.settle, prologue, background, core, lambda: post_products(NP - 1))

        @block.scalar
        def _(act):
            tally = Tally(act)
            at = {}

            def full(u):
                act.wait_ge(pe_act[BANK[u]], tally(pe_act[BANK[u]]))
                return bank(u)

            def both(ins, u, ready):
                ins.then_inc(act_step, 1)
                act.wait_ge(act_step, tally(act_step))
                act.sem_inc(bank_free[BANK[u]], 1)
                act.sem_inc(ready, 1)

            def free(ins, u):
                ins.then_inc(bank_free[BANK[u]], 1)

            def halves(ps):
                return ps[:].rearrange("p (e n) -> p e n", e=2)

            def prologue():
                act.sem_inc(scores_free, 4)
                act.sem_inc(h_kept, 1)
                act.sem_inc(out_stored, 16)
                act.wait_ge(const_act, tally(const_act))
                ps = full("scale_k.0")
                for e in range(2):
                    rows = slice(DH * e, DH * e + DH)
                    src = ps[rows, 0:H * MEM].rearrange("p (f e m) -> p f e m", e=2, m=MEM)[:, :, e, :]
                    ins = act.copy(k_t[rows, :, 0:MEM], src)
                free(ins, "scale_k.0")
                free(act.copy(head_back[:], full("scale_k.1")[:, 0:2 * P].rearrange("p (f n) -> p f n", f=2)), "scale_k.1")

            def copy_scores(s):
                act.wait_ge(scores_free, tally(scores_free))
                for k in range(2):
                    n = cols(2 * ORDER[s] + k)
                    act.wait_ge(score_full[k], tally(score_full[k]))
                    ins = act.copy(scores[:, s % 4, k, 0:n], score_ps[k][:, 0:n])
                    if k == 0:
                        ins.then_inc(score_free[0], 1)
                ins.then_inc(act_step, 1)
                act.wait_ge(act_step, tally(act_step))
                act.sem_inc(score_free[1], 1)
                act.sem_inc(scores_copied, 1)
                act.sem_inc(by_row_free[s % 2], 1)

            def exponentials(s):
                act.wait_ge(max_ready, tally(max_ready))
                for k in range(2):
                    b = 2 * ORDER[s] + k
                    n = cols(b)
                    kind = plan(b)[0]
                    act.activation(probs[:, s % 2, k, 0:n], scores[:, s % 4, k, 0:n], ACT.Exp,
                                   bias=neg_max[:, s % 2, k:k + 1], scale=-1.0 if kind == "low" else 1.0,
                                   accum_out=total[:, s % 2, k:k + 1] if kind == "all" else None).then_inc(exp_ready, 1)

            def normalise_mix(s):
                act.wait_ge(inv_ready, tally(inv_ready))
                for k in range(2):
                    act.mul(mix_n[:, s % 2, k, :], post_mix[:], inv_total[:, s % 2, k:k + 1]).then_inc(mix_ready, 1)

            def copy_probs(s):
                for k in range(2):
                    b = 2 * ORDER[s] + k
                    n = cols(b)
                    act.wait_ge(pt_full[k], tally(pt_full[k]))
                    for t, j0 in enumerate(range(0, n, P)):
                        m = min(P, n - j0)
                        src = pt_ps[k][0:m, P * t:P * t + P].rearrange("p (r h) -> p h r", h=H)
                        dst = (pt0[0:m, :, R * b:R * b + R], pt1[0:m, :, R * b - I1:R * b - I1 + R] if b >= NB // 2 - 1 else None,
                               pt_rest)[t]
                        ins = act.copy(dst, src)
                    ins.then_inc(pt_free[k], 1)

            def core(s, first, last):
                if s is None:
                    copy_scores(0)
                    copy_scores(1)
                    exponentials(0)
                    return
                if not (s == 0 and first):
                    copy_probs((s - 1) % NP)
                if s + 2 < NP or not last:
                    copy_scores((s + 2) % NP)
                at["slot"], at["more"] = s, s + 1 < NP or not last

            def normalise(w, src):
                act.wait_ge(rstd_ready, tally(rstd_ready))
                for t in range(TT):
                    act.activation(xn[:, t], src[:, t], ACT.Identity, bias=shift[:, w, t:t + 1], scale=rstd[:, w, t:t + 1]
                                   ).then_inc(xn_ready, 1)

            def background(step, i, lo=0, hi=1):
                if step == "softmax":
                    normalise_mix(at["slot"])
                    if at["more"]:
                        exponentials((at["slot"] + 1) % NP)
                if step in ("dots1", "dots0"):
                    act.wait_ge(q_root_ready, tally(q_root_ready))
                if step == "dots1":
                    for h in range(H):
                        u = f"dots1.{h}"
                        ps = full(u)
                        ins = act.mul(dots1[:, h, :], ps[:, 0:J], q_scale(1, h))
                        both(ins, u, dots_ready) if h == H - 1 else free(ins, u)
                if step == "dots0":
                    for n in range(8):
                        u = f"dots0.{n}"
                        ps = full(u)
                        h = 4 * (n // 2) + n % 2
                        for e in range(2):
                            ins = act.mul(dots0[:, h + 2 * e, :], ps[:, J0 * e:J0 * e + J0], q_scale(0, h + 2 * e))
                        both(ins, u, dots_ready) if n == 7 else free(ins, u)
                if step == "norms_q":
                    ps = full(step)
                    for t in range(TT):
                        ins = act.copy(qscale[:, t], ps[:, P * t:P * t + P].rearrange("p (g r) -> p g r", g=4)[:, :, 0:4])
                    both(ins, step, sums_ready)
                if step == "norms_k":
                    ps = full(step)
                    both(act.copy(norm_rows, ps[:, 0:TT * P].rearrange("p (t n) -> p t n", t=TT)), step, sums_ready)
                if step == "k_norms":
                    free(act.copy(norm_cols, full("k_norms")[:, 0:N]), "k_norms")
                if step == "v":
                    for n in range(lo, hi):
                        u = f"v.{n}"
                        ps = full(u)
                        jt, half = divmod(n, 2)
                        if n == 4:
                            for half in range(2):
                                ins = act.copy(v_rest[:, 512 * half:512 * half + 512], ps[32 * half:32 * half + REST, :])
                            free(ins, u)
                            continue
                        ins = act.copy(v_sb[:, jt, 512 * half:512 * half + 512], ps[:])
                        if n != 1:
                            free(ins, u)
                            continue
                        ins.then_inc(act_step, 1)
                        act.wait_ge(act_step, tally(act_step))
                        act.sem_inc(bank_free[BANK[u]], 1)
                        act.dma_start(v_sb[0:MEM, 0, :].rearrange("m (h d) -> m h d", h=H),
                                      mem_v.rearrange("h m d -> m h d")).then_inc(mem_v_here, 16)
                if step == "gate":
                    for n in range(lo, hi):
                        u = f"gate.{n}"
                        ps = full(u)
                        for e in range(2):
                            f = 2 * n + e
                            ins = act.activation(gate_t[:, f, :], ps[:, N * e:N * e + N], ACT.Tanh,
                                                 bias=half_bg[:, f:f + 1], scale=0.5)
                        both(ins, u, gates_ready) if n == FT // 2 - 1 else free(ins, u)
                if step == "norm2":
                    normalise(1, h_mid)
                if step == "xn2_t":
                    u = "xn2_t"
                    ps = full(u)
                    act.wait_ge(out_stored, tally(out_stored, 16))
                    both(act.copy(xn2_t[:], halves(ps)), u, xn2_done)
                if step == "edges":
                    if lo == 0:
                        act.wait_ge(h_kept, tally(h_kept))
                    for k, dst in ((0, h_new[:]), (1, abs_v))[lo:hi]:
                        u = f"edges.{k}"
                        ps = full(u)
                        ins = act.activation(dst, halves(ps), ACT.Abs, scale=0.5)
                        both(ins, u, abs_ready) if k == 1 else free(ins, u)
                if step == "ffn_up":
                    for n in range(lo, hi):
                        u = f"ffn_up.{n}"
                        ps = full(u)
                        for e in range(2):
                            f = 2 * n + e
                            ins = act.activation(wide[:, f, :], ps[:, N * e:N * e + N], ACT.Relu, bias=b1_sb[:, f:f + 1])
                        free(ins, u)
                if step == "norm1":
                    normalise(0, h_new)
                if step == "xn_t":
                    free(act.copy(xn_t[:, :, MEM:J], halves(full("xn_t"))), "xn_t")
                if step in ("q", "k"):
                    dst = q_t if step == "q" else k_t[:, :, MEM:J]
                    for n in range(lo, hi):
                        u = f"{step}.{n}"
                        ps = full(u)
                        act.copy(dst[:, 2 * n:2 * n + 2], halves(ps))
                        free(act.activation(squares[step][:, 2 * n:2 * n + 2], halves(ps), ACT.Square), u)
                if step in ("sum_q", "sum_k"):
                    n = ("sum_q", "sum_k").index(step)
                    ps = full(step)
                    free(act.copy((sums_q, sums_k)[n], ps[:, 0:N]), step)

            run(act, tally.settle, prologue, background, core, lambda: copy_probs(NP - 1))
            act.wait_ge(out_stored, tally(out_stored, 16))

        @block.vector
        def _(dve):
            tally = Tally(dve)

            def full(u):
                dve.wait_ge(pe_dve[BANK[u]], tally(pe_dve[BANK[u]]))
                return bank(u)

            def prologue():
                dve.sem_inc(h_mid_free, 1)
                dve.wait_ge(const_dve, tally(const_dve))
                mem = slice(0, H * MEM)
                dve.scalar_tensor_tensor(out=dots0[mem, 1, 0:DH], in0=dots1[mem, 5, 0:DH], scalar=1.0,
                                         in1=dots1[mem, 5, 0:DH], op0=ALU.mult, op1=ALU.mult,
                                         accum_out=total[mem, 0, 0:1]).then_inc(mv_ready, 1)

            def find_cut(s):
                dve.wait_ge(scores_ready, tally(scores_ready, 2))
                p = ORDER[s]
                plans = [plan(2 * p + k) for k in range(2)]
                src = [scores[:, s % 4, k, 0:cols(2 * p + k)] for k in range(2)]
                wrk = [work[:, k, 0:cols(2 * p + k)] for k in range(2)]
                for k in range(2):
                    dve.max(top8[:, k, :], src[k]).then_inc(block_step[k], 1)
                for k in range(2):
                    dve.wait_ge(block_step[k], tally(block_step[k]))
                    if plans[k][0] == "low":
                        dve.tensor_scalar(src[k], src[k], -1.0, None, ALU.mult).then_inc(block_step[k], 1)
                for k in range(2):
                    if plans[k][0] == "low":
                        dve.wait_ge(block_step[k], tally(block_step[k]))
                dve.tensor_scalar(neg_max[:, s % 2, :], top8[:, :, 0], -1.0, None, ALU.mult).then_inc(max_ready, 1)
                for k in range(2):
                    if plans[k][0] == "low":
                        dve.max(cut8[:, k, :], src[k]).then_inc(block_step[k], 1)
                for r in range(1, 8):
                    for k in range(2):
                        if r < plans[k][1]:
                            eight = top8 if r == 1 and plans[k][0] == "top" else cut8
                            if eight is cut8:
                                dve.wait_ge(block_step[k], tally(block_step[k]))
                            dve.match_replace(wrk[k], eight[:, k, :], src[k] if r == 1 else wrk[k], TAKEN
                                              ).then_inc(block_step[k], 1)
                    for k in range(2):
                        if r < plans[k][1]:
                            dve.wait_ge(block_step[k], tally(block_step[k]))
                            dve.max(cut8[:, k, :], wrk[k]).then_inc(block_step[k], 1)

            def cut_and_sum(s):
                p = ORDER[s]
                dve.wait_ge(exp_ready, tally(exp_ready, 2))
                for k in range(2):
                    kind, rounds, at = plan(2 * p + k)
                    n = cols(2 * p + k)
                    if kind == "all":
                        continue
                    dve.wait_ge(block_step[k], tally(block_step[k]))
                    pr = probs[:, s % 2, k, 0:n]
                    dve.scalar_tensor_tensor(out=pr, in0=scores[:, s % 4, k, 0:n], scalar=cut8[:, k, at:at + 1], in1=pr,
                                             op0=ALU.is_ge if kind == "top" else ALU.is_le, op1=ALU.mult,
                                             accum_out=total[:, s % 2, k:k + 1]).then_inc(block_step[k], 1)
                for k in range(2):
                    if plan(2 * p + k)[0] != "all":
                        dve.wait_ge(block_step[k], tally(block_step[k]))
                dve.reciprocal(inv_total[:, s % 2, :], total[:, s % 2, :]).then_inc(inv_ready, 1)
                dve.sem_inc(scores_free, 1)

            def core(s, first, last):
                if s is None:
                    find_cut(0)
                    return
                cut_and_sum(s)
                if s + 1 < NP or not last:
                    find_cut((s + 1) % NP)

            def moments(w, src):
                for t in range(TT):
                    dve.bn_stats(stats[:, t, :], src[:, t]).then_inc(dve_step, 1)
                for t in range(TT):
                    dve.wait_ge(dve_step, tally(dve_step))
                    dve.bn_aggr(mv[:, w, t, :], stats[:, t, :]).then_inc(mv_ready, 1)

            def gate_heads():
                for g in range(FT // 2):
                    u = f"values.{g}"
                    ps = full(u)
                    fs = slice(2 * g, 2 * g + 2)
                    if g == 0:
                        dve.wait_ge(gates_ready, tally(gates_ready))
                    dve.scalar_tensor_tensor(out=heads_t[:, fs, :], in0=gate_t[:, fs, :], scalar=1.0,
                                             in1=ps[:].rearrange("p (f n) -> p f n", n=N), op0=ALU.add, op1=ALU.mult
                                             ).then_inc(bank_free[BANK[u]], 1)

            def background(step, i, lo=0, hi=1):
                if step == "gate_heads":
                    gate_heads()
                if step == "project":
                    ps = full("project")
                    dve.wait_ge(h_moved, tally(h_moved))
                    dve.tensor_tensor(h_mid[:], h_mid[:], ps[:].rearrange("p (t d) -> p t d", t=TT), ALU.add).then_inc(dve_step, 1)
                    dve.wait_ge(dve_step, tally(dve_step))
                    dve.sem_inc(bank_free[BANK["project"]], 1)
                    moments(1, h_mid)
                if step == "moments":
                    dve.wait_ge(h_ready, tally(h_ready))
                    moments(0, h_new)
                if step == "ffn_down" and hi == TT:
                    u = "ffn_down"
                    ps = full(u)
                    dve.wait_ge(h_mid_ready, tally(h_mid_ready))
                    dve.tensor_tensor(out_sb[:], h_mid[:], ps[:].rearrange("p (t d) -> p t d", t=TT), ALU.add
                                      ).then_inc(dve_step, 1)
                    dve.wait_ge(dve_step, tally(dve_step))
                    dve.sem_inc(bank_free[BANK[u]], 1)
                    dve.sem_inc(out_ready, 1)
                    dve.sem_inc(h_mid_free, 1)
                if step == "scale_k":
                    for n in range(FT // 2):
                        u = f"scale_k.{n}"
                        ps = full(u)
                        keys = k_t[:, n:n + 5:4, MEM:J]
                        dve.tensor_tensor(keys, keys,
                                          ps[:].rearrange("p (e n) -> p e n", e=2), ALU.mult).then_inc(bank_free[BANK[u]], 1)

            run(dve, tally.settle, prologue, background, core)


_INS = ["x", "L0_tok_scharr", "L0_attn_Wq", "L0_attn_Wk", "L0_attn_Wv", "L0_attn_W_pre_th", "L0_attn_W_post_th", "L0_attn_mem_k",
        "L0_attn_mem_v", "L0_attn_head_scale_params", "L0_attn_Wg", "L0_attn_bg", "L0_attn_Wo", "L0_ffn_w1", "L0_ffn_b1",
        "L0_ffn_w2", "L0_ffn_b2"]


def kernel(**inputs):
    import numpy as _np
    import concourse.bacc as _bacc
    from concourse import mybir as _mybir
    from concourse.bass_utils import run_bass_kernel_spmd as _run

    nc = _bacc.Bacc("TRN2", target_bir_lowering=False, num_devices=1)
    arrays, args = {}, []
    for name in _INS:
        a = _np.ascontiguousarray(inputs[name])
        arrays[f"in_{name}_dram"] = a
        args.append(nc.dram_tensor(f"in_{name}_dram", a.shape, _mybir.dt.from_np(a.dtype), kind="ExternalInput").ap())
    n, _, rows, width = inputs["x"].shape
    out = nc.dram_tensor("out_dram", (n, rows, width), _mybir.dt.float32, kind="ExternalOutput").ap()
    vit_layer(nc, *args, out)
    r = _run(nc, [arrays], core_ids=[0])
    return r.results[0]["out_dram"]
```

```python
from contextlib import ExitStack

import concourse.bass as bass
from concourse import mybir

F32 = mybir.dt.float32
ALU = mybir.AluOpType
ACT = mybir.ActivationFunctionType

P = 128
GRAY = (0.2989, 0.587, 0.114)
LN_EPS = 1e-5
NORM_EPS = 1e-12
QK_SCALE = 10.0
TOPK = 64
MASKED = -1e30
TAKEN = -3e38

SCHEDULE = {
    0: (("next", "load_x"), ("cur", "softmax"), ("prev", "values", 0, 4), ("prev", "gate_heads"), ("next", "gray"),
        ("prev", "move_h"), ("cur", "keep_h")),
    1: (("cur", "softmax"), ("cur", "v", 0, 4)),
    2: (("cur", "softmax"), ("cur", "v", 4, 5), ("next", "edges", 0, 1)),
    3: (("cur", "softmax"), ("next", "edges", 1, 2), ("cur", "gate", 0, 1)),
    4: (("cur", "softmax"), ("cur", "gate", 1, 4), ("next", "moments"), ("next", "norm1")),
    5: (("cur", "softmax"), ("prev", "project"), ("next", "xn_t")),
    6: (("cur", "softmax"), ("next", "q", 0, 3), ("prev", "add_project")),
    7: (("cur", "softmax"), ("prev", "norm2"), ("next", "q", 3, 4), ("next", "k", 0, 2), ("prev", "xn2_t")),
    8: (("cur", "softmax"), ("prev", "add_b2"), ("next", "k", 2, 4), ("next", "sum_q")),
    9: (("cur", "softmax"), ("next", "sum_k"), ("next", "norms_q"), ("next", "norms_k"), ("next", "root_k", 0, 2),
        ("prev", "ffn_up", 0, 1)),
    10: (("cur", "softmax"), ("next", "root_q", 1, 2), ("prev", "ffn_up", 1, 2)),
    11: (("cur", "softmax"), ("next", "root_q", 0, 1), ("next", "k_norms"), ("prev", "ffn_up", 2, 3),
        ("next", "scale_k", 0, 4), ("prev", "ffn_up", 3, 4)),
    12: (("next", "dots1", 0, 3), ("cur", "softmax"), ("next", "dots1", 3, 16)),
    13: (("next", "dots0", 0, 3), ("cur", "softmax"), ("next", "dots0", 3, 8)),
    14: (("cur", "softmax"), ("prev", "ffn_down", 0, 1)),
    15: (("cur", "softmax"), ("prev", "ffn_down", 1, 2), ("prev", "add_output")),
}


class Tally:

    def __init__(self, eng):
        self.eng, self.seen = eng, {}

    def __call__(self, sem, events=1):
        self.seen[sem.name] = (sem, self.seen.get(sem.name, (sem, 0))[1] + events)
        return self.seen[sem.name][1]

    def peek(self, sem, events=1):
        return self.seen.get(sem.name, (sem, 0))[1] + events

    def settle(self):
        for sem, events in self.seen.values():
            self.eng.sem_inc(sem, -events)
        self.seen = {}


def vit_layer(nc, x, scharr, Wq, Wk, Wv, W_pre, W_post, mem_k, mem_v, head_scale, Wg, bg, Wo, w1, b1, w2, b2, out):
    B, C, N, D = x.shape
    H, MEM, DH = mem_k.shape
    HD = H * DH
    KT = D // P
    TT = N // P
    FT = HD // P
    WF = w1.shape[1] // P
    J = MEM + N
    R = P // H
    NB = N // R
    NP = NB // 2
    J0 = MEM + P
    I1 = P - R
    REST = J - 2 * P
    assert H * R == P and TT == 2 and KT == 2 and 2 * DH == P and WF == FT == 8 and 0 < REST <= R

    def cols(b):
        return MEM + R * (b + 1)

    ORDER = [p for n in range(NP // 2) for p in (NP - 1 - n, n)]

    def score_parts(p):
        n = cols(2 * p + 1)
        return [(0, (0, 1), n)] if 2 * n <= 512 else [(0, (0,), n - R), (n - R, (1,), n)]

    def plan(b):
        n = cols(b)
        if n <= TOPK:
            return "all", 0, 0
        drop = n - TOPK
        low = drop // 8 + 1
        return ("low", low, drop % 8) if low < 8 else ("top", TOPK // 8, 7)

    with ExitStack() as ctx:
        def sb(name, shape):
            return ctx.enter_context(nc.sbuf_tensor(name, shape, F32))

        def sem(name):
            return ctx.enter_context(nc.semaphore(name))

        wq_sb, wk_sb, wv_sb, wg_sb = (sb(f"w{c}_sb", [P, KT, HD]) for c in "qkvg")
        w1_sb = sb("w1_sb", [P, KT, WF * P])
        w2_sb = sb("w2_sb", [P, WF, D])
        wo_sb = sb("wo_sb", [P, FT, D])
        half_bg = sb("half_bg", [P, FT])
        b1_sb = sb("b1_sb", [P, WF])
        b2_sb = sb("b2_sb", [P, D])
        ident = sb("ident", [P, P])
        bands = sb("bands", [P, 2, 3, P])
        pre_mix = sb("pre_mix", [P, P])
        post_mix = sb("post_mix", [P, P])
        future = sb("future", [P, R])
        head_sel = sb("head_sel", [P, 2, 4, 32])
        head_back = sb("head_back", [P, 2, P])
        power = sb("power", [P, 1])
        x_in = sb("x_in", [P, C, TT, D])
        gray = sb("gray", [P, TT, D + 2])
        edge_hi = sb("edge_hi", [P, HD])
        edge_lo = sb("edge_lo", [P, 2, TT, P])
        h_new = sb("h_new", [P, TT, D])
        h_cur = sb("h_cur", [P, TT, D])
        h_mid = sb("h_mid", [P, TT, D])
        xn = sb("xn", [P, TT, D])
        xn_t = sb("xn_t", [P, KT, J])
        xn2_t = sb("xn2_t", [P, KT, N])
        out_sb = xn2_t
        q_t = sb("q_t", [P, FT, N])
        k_t = sb("k_t", [P, FT, J])
        v_sb = sb("v_sb", [P, 2, HD])
        gate_t = sb("gate_t", [P, FT, N])
        wide = sb("wide", [P, FT, N])
        dots0 = sb("dots0", [P, H, J0])
        dots1 = sb("dots1", [P, H, J])
        by_row = sb("by_row", [P, 2, 2, J])
        scores = sb("scores", [P, 4, 2, J])
        probs = sb("probs", [P, 2, 2, J])
        work = sb("work", [P, 2, J])
        mix_n = sb("mix_n", [P, 2, 2, P])
        pt0 = sb("pt0", [P, H, N])
        pt1 = sb("pt1", [P, H, N - I1])
        heads_t = sb("heads_t", [P, FT, N])
        stats = sb("stats", [P, TT, 6])
        mv = sb("mv", [P, 2, TT, 2])
        rstd = sb("rstd", [P, 2, TT])
        shift = sb("shift", [P, 2, TT])
        qscale = sb("qscale", [P, TT, 4, 4])
        top8 = sb("top8", [P, 2, 2, 8])
        cut8 = sb("cut8", [P, 2, 8])
        neg_max = sb("neg_max", [P, 2, 2])
        total = sb("total", [P, 2, 2])
        inv_total = sb("inv_total", [P, 2, 2])

        halo = edge_hi[32:35, 0:TT * D].rearrange("p (t d) -> p t d", t=TT)
        halo_w = edge_lo[32:35]
        abs_v = wide[:, 0:2, :]
        squares = {"q": wide, "k": heads_t}
        sums_q, sums_k = xn[:, 0, :], xn[:, 1, :]
        norm_rows = xn[:, 0, :].rearrange("p (t n) -> p t n", t=TT)
        norm_cols = xn[:, 1, :]

        def q_scale(t, h):
            f = h // 2
            r = 2 * (f // 4) + h % 2
            return qscale[:, t, f % 4, r:r + 1]

        v_rest = edge_hi[0:REST, :]
        pt_rest = edge_lo[0:REST].rearrange("p a b c -> p (a b c)")[:, 0:H * R].rearrange("p (h r) -> p h r", h=H)

        banks = [ctx.enter_context(nc.psum_tensor(f"bank{i}", [P, 512], F32)) for i in range(4)]
        score_ps = [ctx.enter_context(nc.psum_tensor(f"score_ps{i}", [P, 512], F32)) for i in range(2)]
        pt_ps = [ctx.enter_context(nc.psum_tensor(f"pt_ps{i}", [P, 512], F32)) for i in range(2)]

        loaded_pool = sem("loaded_pool")
        loaded_pe = sem("loaded_pe")
        loaded_wq = sem("loaded_wq")
        loaded_wk = sem("loaded_wk")
        loaded_filters = sem("loaded_filters")
        loaded_halo_w = sem("loaded_halo_w")
        taps_ready = sem("taps_ready")
        bands_ready = sem("bands_ready")
        zeroed = sem("zeroed")
        gray_halo = sem("gray_halo")
        const_pe = sem("const_pe")
        const_act = sem("const_act")
        const_dve = sem("const_dve")
        pool_step = sem("pool_step")
        act_step = sem("act_step")
        dve_step = sem("dve_step")
        block_step = [sem(f"block_step{k}") for k in range(2)]
        max_step = [sem(f"max_step{k}") for k in range(2)]
        sum_step = sem("sum_step")
        pe_act = [sem(f"bank{i}_full_for_act") for i in range(4)]
        pe_dve = [sem(f"bank{i}_full_for_dve") for i in range(4)]
        bank_free = [sem(f"bank{i}_free") for i in range(4)]
        x_here = sem("x_here")
        x_used = sem("x_used")
        gray_ready = sem("gray_ready")
        halo_here = sem("halo_here")
        abs_ready = sem("abs_ready")
        h_ready = sem("h_ready")
        h_mid_ready = sem("h_mid_ready")
        mv_ready = sem("mv_ready")
        rstd_ready = sem("rstd_ready")
        xn_ready = sem("xn_ready")
        sums_ready = sem("sums_ready")
        k_root_ready = sem("k_root_ready")
        q_root_ready = sem("q_root_ready")
        dots_ready = sem("dots_ready")
        mem_v_here = sem("mem_v_here")
        gates_ready = sem("gates_ready")
        xn2_done = sem("xn2_done")
        h_kept = sem("h_kept")
        h_moved = sem("h_moved")
        h_mid_free = sem("h_mid_free")
        scores_copied = sem("scores_copied")
        out_ready = sem("out_ready")
        out_stored = sem("out_stored")
        by_row_here = [sem(f"by_row_here{i}") for i in range(2)]
        by_row_free = [sem(f"by_row_free{i}") for i in range(2)]
        score_full = [sem(f"score_full{r}") for r in range(2)]
        score_free = [sem(f"score_free{k}") for k in range(2)]
        scores_ready = sem("scores_ready")
        scores_free = sem("scores_free")
        max_ready = sem("max_ready")
        exp_ready = sem("exp_ready")
        inv_ready = sem("inv_ready")
        mix_ready = sem("mix_ready")
        pt_full = [sem(f"pt_full{k}") for k in range(2)]
        pt_free = [sem(f"pt_free{k}") for k in range(2)]

        block = ctx.enter_context(nc.Block())

        ONE_BANK = ("project", "xn_t", "xn2_t", "sum_q", "sum_k", "norms_q", "norms_k", "k_norms")
        UNITS = []
        for s in range(NP):
            for _, step, *part in SCHEDULE[s]:
                if step in ONE_BANK or step == "ffn_down" and part[0] == 0:
                    UNITS.append(step)
                elif part and step not in ("ffn_down", "root_q", "root_k"):
                    UNITS.extend(f"{step}.{n}" for n in range(*part))
        BANK = {u: i % 4 for i, u in enumerate(UNITS)}

        def bank(u):
            return banks[BANK[u]]

        def run(eng, settle, prologue, background, core, after=None):
            def batch(first, last, i):
                for s in range(NP):
                    core(s, first, last)
                    for whose, step, *part in SCHEDULE[s]:
                        if not (whose == "prev" and first or whose == "next" and last):
                            background(step, i, *part)
                settle()

            prologue()
            for s in range(NP):
                for whose, step, *part in SCHEDULE[s]:
                    if whose == "next":
                        background(step, None, *part)
            core(None, True, False)
            settle()
            batch(True, False, 0)
            with eng.Fori(1, B - 1) as i:
                batch(False, False, i)
            batch(False, True, B - 1)
            if after:
                after()
            for s in range(NP):
                for whose, step, *part in SCHEDULE[s]:
                    if whose == "prev":
                        background(step, B, *part)

        @block.sync
        def _(sp):
            tally = Tally(sp)

            def load_halo():
                sp.wait_ge(gray_halo, tally(gray_halo))
                for dx in range(3):
                    sp.dma_start(halo[dx:dx + 1, 0, :], gray[0:1, 1, dx:dx + D]).then_inc(halo_here, 16)
                    sp.dma_start(halo[dx:dx + 1, 1, :], gray[P - 1:P, 0, dx:dx + D]).then_inc(halo_here, 16)

            def prologue():
                for r in range(2):
                    sp.sem_inc(by_row_free[r], 1)
                with nc.allow_non_contiguous_dma(reason="weights of a few hundred words, once"):
                    sp.dma_start(dots1[:, 3, 0:18],
                                   scharr.rearrange("a b c d -> (a b c d)").partition_broadcast(P)).then_inc(loaded_filters, 16)
                    sp.wait_ge(zeroed, tally(zeroed))
                    for k in range(2):
                        for t, dy, col in ((0, 2, P - 1), (1, 0, 0)):
                            sp.dma_start(halo_w[:, k, t, col:col + 1],
                                           scharr[k, 0, dy:dy + 1, :].rearrange("a b -> b a")).then_inc(loaded_halo_w, 16)
                    sp.dma_start(wq_sb[:], Wq.rearrange("(k p) n -> p k n", p=P)).then_inc(loaded_wq, 16)
                    load_halo()
                    for r in range(R):
                        for w, t in ((W_pre, pre_mix), (W_post, post_mix)):
                            sp.dma_start(t[H * r:H * r + H, H * r:H * r + H],
                                           w.rearrange("h g -> g h")).then_inc(loaded_pool, 16)
                    sp.dma_start(b2_sb[:], b2.partition_broadcast(P)).then_inc(loaded_pool, 16)
                    sp.dma_start(b1_sb[:], b1.rearrange("(f p) -> p f", p=P)).then_inc(loaded_pool, 16)
                    sp.dma_start(half_bg[:], bg.rearrange("(f p) -> p f", p=P)).then_inc(loaded_pool, 16)
                    for e in range(2):
                        sp.dma_start(dots1[DH * e:DH * e + DH, 4, 0:FT],
                                       head_scale.rearrange("a (f e) b c -> (a b c) e f", e=2)[0, e].partition_broadcast(DH)
                                       ).then_inc(loaded_pool, 16)
                    sp.dma_start(wo_sb[:], Wo.rearrange("(f p) n -> p f n", p=P)).then_inc(loaded_pool, 16)
                    for e in range(2):
                        sp.dma_start(dots1[0:H * MEM, 5 + e, 0:DH],
                                       mem_k.rearrange("h m d -> (h m) d")).then_inc(loaded_pool, 16)
                sp.dma_start(wk_sb[:], Wk.rearrange("(k p) n -> p k n", p=P)).then_inc(loaded_wk, 16)
                for dst, src in ((wv_sb, Wv), (wg_sb, Wg), (w1_sb, w1)):
                    sp.dma_start(dst[:], src.rearrange("(k p) n -> p k n", p=P)).then_inc(loaded_pe, 16)
                sp.dma_start(w2_sb[:], w2.rearrange("(k p) n -> p k n", p=P)).then_inc(loaded_pe, 16)

            def regroup(s):
                r = s % 2
                p = ORDER[s]
                if s < 2:
                    sp.wait_ge(dots_ready, tally(dots_ready))
                sp.wait_ge(by_row_free[r], tally(by_row_free[r]))
                n = cols(2 * p + 1)
                for k in range(2):
                    b = 2 * p + k
                    src = dots0 if b < NB // 2 else dots1
                    i0 = R * (b % (NB // 2))
                    sp.dma_start(by_row[:, r, k, 0:n], src[i0:i0 + R, :, 0:n]).then_inc(by_row_here[r], 16)

            def background(step, i, lo=0, hi=1):
                if step == "gray" and i is not None:
                    load_halo()
                if step == "add_output":
                    sp.wait_ge(out_ready, tally(out_ready))
                    sp.dma_start(out[i - 1].rearrange("(t p) d -> p t d", p=P), out_sb[:]).then_inc(out_stored, 16)

            def core(s, first, last):
                if s is None:
                    for n in range(4):
                        regroup(n)
                elif s + 4 < NP or not last:
                    regroup((s + 4) % NP)

            run(sp, tally.settle, prologue, background, core)

        @block.gpsimd
        def _(pool):
            tally = Tally(pool)

            def chain(ins):
                ins.then_inc(pool_step, 1)
                pool.wait_ge(pool_step, tally(pool_step))

            def make_gray():
                pool.wait_ge(x_here, tally(x_here, 16))
                inner = gray[:, :, 1:D + 1]
                chain(pool.tensor_scalar(inner, x_in[:, 0], GRAY[0], 1.0, ALU.mult, ALU.mult))
                for c in (1, 2):
                    chain(pool.tensor_scalar(x_in[:, c], x_in[:, c], GRAY[c], 1.0, ALU.mult, ALU.mult))
                    chain(pool.tensor_tensor(inner, inner, x_in[:, c], ALU.add))
                pool.sem_inc(gray_ready, 1)
                pool.sem_inc(x_used, 1)
                pool.sem_inc(gray_halo, 1)

            def prologue():
                for t in (edge_lo, pre_mix, post_mix):
                    chain(pool.memset(t[:], 0.0))
                pool.sem_inc(zeroed, 1)
                chain(pool.memset(dots1[:, 0:3, 0:P], 0.0))
                for dy in range(3):
                    chain(pool.affine_select(out=dots1[:, dy, 0:P], in_=dots1[:, dy, 0:P], compare_op=ALU.not_equal,
                                             fill=1.0, base=1 - dy, pattern=[[-1, P]], channel_multiplier=1))
                pool.sem_inc(taps_ready, 1)
                chain(pool.memset(gray[:], 0.0))
                make_gray()
                for t in (ident, future, head_sel, pt0, pt1, xn_t):
                    chain(pool.memset(t[:], 0.0))
                chain(pool.memset(power[:], -0.5))
                for f in range(2):
                    for e in range(2):
                        r = 2 * f + e
                        chain(pool.memset(head_sel[DH * e:DH * e + DH, f, :, r:r + 1], 1.0))
                chain(pool.affine_select(out=ident[:], in_=ident[:], compare_op=ALU.not_equal, fill=1.0,
                                         base=0, pattern=[[-1, P]], channel_multiplier=1))
                chain(pool.affine_select(out=future[:], in_=future[:], compare_op=ALU.is_ge, fill=MASKED,
                                         base=0, pattern=[[-H, R]], channel_multiplier=1))

            def constants():
                pool.wait_ge(loaded_pool, tally(loaded_pool, 16 * (2 * R + 3 + 2 + 1 + 2)))
                chain(pool.tensor_scalar(half_bg[:], half_bg[:], 0.5, 1.0, ALU.mult, ALU.mult))
                for f in range(FT):
                    chain(pool.tensor_scalar(wo_sb[:, f, :], wo_sb[:, f, :], dots1[:, 4, f:f + 1], 0.5, ALU.mult, ALU.mult))
                pool.sem_inc(const_dve, 1)
                pool.wait_ge(mv_ready, tally(mv_ready))
                mem = slice(0, H * MEM)
                chain(pool.tensor_scalar(total[mem, 0, 0:1], total[mem, 0, 0:1], NORM_EPS * NORM_EPS, 1.0, ALU.max, ALU.mult))
                chain(pool.tensor_tensor(total[mem, 0, 1:2], total[mem, 0, 0:1], power[mem, 0:1], ALU.pow))
                for e in range(2):
                    chain(pool.tensor_scalar(dots0[mem, 0, DH * e:DH * e + DH], dots1[mem, 5 + e, 0:DH], total[mem, 0, 1:2], 1.0,
                                             ALU.mult, ALU.mult))
                pool.sem_inc(const_pe, 1)
                pool.sem_inc(const_act, 1)

            def normalise_prepare(w):
                pool.wait_ge(mv_ready, tally(mv_ready, 2))
                chain(pool.tensor_scalar(rstd[:, w], mv[:, w, :, 1], LN_EPS, 1.0, ALU.add, ALU.mult))
                chain(pool.tensor_tensor(rstd[:, w], rstd[:, w], power[:].to_broadcast([P, TT]), ALU.pow))
                chain(pool.tensor_tensor(shift[:, w], mv[:, w, :, 0], rstd[:, w], ALU.mult))
                chain(pool.tensor_scalar(shift[:, w], shift[:, w], -1.0, 1.0, ALU.mult, ALU.mult))
                pool.sem_inc(rstd_ready, 1)

            def inverse_root(norms):
                chain(pool.tensor_scalar(norms, norms, NORM_EPS * NORM_EPS, 1.0, ALU.max, ALU.mult))
                chain(pool.tensor_tensor(norms, norms, power[:].unsqueeze(2).to_broadcast([P, 4, 4]), ALU.pow))

            def mask_future(s):
                pool.wait_ge(scores_copied, tally(scores_copied))
                for k in range(2):
                    n = cols(2 * ORDER[s] + k)
                    own = scores[:, s % 4, k, n - R:n]
                    pool.tensor_tensor(own, own, future[:], ALU.add).then_inc(scores_ready, 1)

            def core(s, first, last):
                if s is None:
                    mask_future(0)
                    mask_future(1)
                elif s + 2 < NP or not last:
                    mask_future((s + 2) % NP)

            def background(step, i, lo=0, hi=1):
                if step == "norm2":
                    normalise_prepare(1)
                if step == "move_h":
                    pool.wait_ge(h_mid_free, tally(h_mid_free))
                    chain(pool.tensor_copy(h_mid[:], h_cur[:]))
                    pool.sem_inc(h_moved, 1)
                if step == "keep_h":
                    chain(pool.tensor_copy(h_cur[:], h_new[:]))
                    pool.sem_inc(h_kept, 1)
                if step == "gray" and i is not None:
                    make_gray()
                if step == "add_b2":
                    pool.wait_ge(xn2_done, tally(xn2_done))
                    for t in range(TT):
                        chain(pool.tensor_tensor(h_mid[:, t], h_mid[:, t], b2_sb[:], ALU.add))
                    pool.sem_inc(h_mid_ready, 1)
                if step == "edges" and hi == 2:
                    pool.wait_ge(abs_ready, tally(abs_ready))
                    chain(pool.tensor_tensor(h_new[:], h_new[:], abs_v, ALU.add))
                    pool.sem_inc(h_ready, 1)
                if step == "norm1":
                    normalise_prepare(0)
                    if i is None:
                        constants()
                if step == "root_k":
                    if lo == 0:
                        pool.wait_ge(sums_ready, tally(sums_ready, 2))
                    for t in range(lo, hi):
                        inverse_root(norm_rows[:, t, :].rearrange("p (g r) -> p g r", g=4)[:, :, 0:4])
                    if hi == TT:
                        pool.sem_inc(k_root_ready, 1)
                if step == "root_q":
                    inverse_root(qscale[:, lo])
                    chain(pool.tensor_scalar(qscale[:, lo], qscale[:, lo], QK_SCALE, 1.0, ALU.mult, ALU.mult))
                    pool.sem_inc(q_root_ready, 1)

            run(pool, tally.settle, prologue, background, core)

        @block.tensor
        def _(pe):
            tally = Tally(pe)

            holder = {}

            def take_bank(u):
                holder[BANK[u]] = u
                pe.wait_ge(bank_free[BANK[u]], tally(bank_free[BANK[u]]))
                return bank(u)

            def copied(u):
                if holder[BANK[u]] == u:
                    pe.wait_ge(bank_free[BANK[u]], tally.peek(bank_free[BANK[u]]))

            def prologue():
                for k in range(2):
                    pe.sem_inc(score_free[k], 1)
                    pe.sem_inc(pt_free[k], 1)
                for i in range(4):
                    pe.sem_inc(bank_free[i], 1)

            def constants():
                pe.wait_ge(const_pe, tally(const_pe))
                ps = take_bank("scale_k.0")
                pe.transpose(ps[:, 0:H * MEM], dots0[0:H * MEM, 0, 0:P], ident[0:H * MEM, 0:H * MEM]
                             ).then_inc(pe_act[BANK["scale_k.0"]], 1)
                ps = take_bank("scale_k.1")
                for f in range(2):
                    mm = pe.transpose(ps[:, P * f:P * f + P], head_sel[:, f].rearrange("p g r -> p (g r)"), ident[:])
                mm.then_inc(pe_act[BANK["scale_k.1"]], 1)

            def score_products(s):
                r = s % 2
                p = ORDER[s]
                pe.wait_ge(by_row_here[r], tally(by_row_here[r], 32))
                pe.wait_ge(score_free[r], tally(score_free[r]))
                for at, ks, n in score_parts(p):
                    mm = pe.matmul(score_ps[r][:, at:at + len(ks) * n], pre_mix[:], by_row[:, r, ks[0]:ks[-1] + 1, 0:n],
                                   start=True, stop=True)
                mm.then_inc(score_full[r], 1)

            def post_products(s):
                for k in range(2):
                    b = 2 * ORDER[s] + k
                    n = cols(b)
                    pe.wait_ge(mix_ready, tally(mix_ready))
                    pe.wait_ge(pt_free[k], tally(pt_free[k]))
                    tiles = [(j, min(j + P, n)) for j in range(0, n, P)]
                    for t, (j0, j1) in enumerate(tiles):
                        last_mm = pe.matmul(pt_ps[k][0:j1 - j0, P * t:P * t + P], probs[:, s % 2, k, j0:j1], mix_n[:, s % 2, k, :],
                                            start=True, stop=True)
                    last_mm.then_inc(pt_full[k], 1)

            def core(s, first, last):
                if s is None:
                    pe.wait_ge(loaded_pe, tally(loaded_pe, 16 * 4))
                    score_products(0)
                    score_products(1)
                    return
                if not (s == 0 and first):
                    post_products((s - 1) % NP)
                if s + 2 < NP or not last:
                    score_products((s + 2) % NP)

            def values():
                for k in range(2):
                    pe.wait_ge(pt_free[k], tally.peek(pt_free[k]))
                pe.wait_ge(mem_v_here, tally(mem_v_here, 16))
                for g in range(FT // 2):
                    u = f"values.{g}"
                    ps = take_bank(u)
                    for f in (2 * g, 2 * g + 1):
                        for n, (vals, pt, i0) in enumerate(((v_sb[:, 0], pt0, 0), (v_sb[:, 1], pt1, I1), (v_rest, pt_rest, N - R))):
                            for e in range(2):
                                h = 2 * f + e
                                o = ps[DH * e:DH * e + DH, N * (f % 2) + i0:N * (f % 2) + N]
                                mm = pe.matmul(o, vals[:, DH * h:DH * h + DH], pt[:, h, :], start=(n == 0), stop=(n == 2))
                    mm.then_inc(pe_dve[BANK[u]], 1)

            def project():
                for g in range(FT // 2):
                    copied(f"values.{g}")
                ps = take_bank("project")
                for t in range(TT):
                    for f in range(FT):
                        mm = pe.matmul(ps[:, D * t:D * t + D], heads_t[:, f, P * t:P * t + P], wo_sb[:, f, :],
                                       start=(f == 0), stop=(f == FT - 1))
                mm.then_inc(pe_dve[BANK["project"]], 1)

            def features(name, w, src, lo, hi):
                for u in range(lo, hi):
                    ps = take_bank(f"{name}.{u}")
                    for e in range(2):
                        f = 2 * u + e
                        for c in range(KT):
                            mm = pe.matmul(ps[:, N * e:N * e + N], w[:, c, P * f:P * f + P], src[:, c],
                                           start=(c == 0), stop=(c == KT - 1))
                    mm.then_inc(pe_act[BANK[f"{name}.{u}"]], 1)

            def sums_of_squares(u):
                for n in range(FT // 2):
                    copied(f"{u[-1]}.{n}")
                ps = take_bank(u)
                for f in range(FT):
                    g = 32 * (f % 4)
                    mm = pe.matmul(ps[g:g + 32, 0:N], head_sel[:, f // 4, 0, :], squares[u[-1]][:, f, :],
                                   start=(f < 4), stop=(f >= 4))
                mm.then_inc(pe_act[BANK[u]], 1)

            def transposes(u, dst_act):
                ps = take_bank(u)
                for c in range(KT):
                    for t in range(TT):
                        mm = pe.transpose(ps[:, N * c + P * t:N * c + P * t + P], xn[:, t, P * c:P * c + P], ident[:])
                mm.then_inc(dst_act[BANK[u]], 1)

            def dots(name, t, heads, n):
                ps = take_bank(name)
                for at, h in enumerate(heads):
                    rows = slice(DH * (h % 2), DH * (h % 2) + DH)
                    mm = pe.matmul(ps[:, n * at:n * at + n], q_t[rows, h // 2, P * t:P * t + P], k_t[rows, h // 2, 0:n],
                                   start=True, stop=True)
                mm.then_inc(pe_act[BANK[name]], 1)

            def background(step, i, lo=0, hi=1):
                if step == "dots1":
                    if lo == 0:
                        for u in range(FT // 2):
                            copied(f"scale_k.{u}")
                    for h in range(lo, hi):
                        dots(f"dots1.{h}", 1, [h], J)
                if step == "values":
                    values()
                if step == "project":
                    project()
                if step == "v":
                    for u in range(lo, min(hi, 4)):
                        ps = take_bank(f"v.{u}")
                        jt, half = divmod(u, 2)
                        for c in range(KT):
                            mm = pe.matmul(ps[:], xn_t[:, c, P * jt:P * jt + P], wv_sb[:, c, 512 * half:512 * half + 512],
                                           start=(c == 0), stop=(c == KT - 1))
                        mm.then_inc(pe_act[BANK[f"v.{u}"]], 1)
                    if hi == 5:
                        ps = take_bank("v.4")
                        for c in range(KT):
                            for g in range(4):
                                mm = pe.matmul(ps[32 * g:32 * g + REST, 0:HD // 4], xn_t[:, c, 2 * P:J],
                                               wv_sb[:, c, HD // 4 * g:HD // 4 * (g + 1)], start=(c == 0), stop=(c == KT - 1))
                        mm.then_inc(pe_act[BANK["v.4"]], 1)
                if step == "gate":
                    features("gate", wg_sb, xn_t[:, :, MEM:J], lo, hi)
                if step == "xn2_t":
                    pe.wait_ge(xn_ready, tally(xn_ready, 2))
                    transposes("xn2_t", pe_act)
                if step == "edges":
                    if i is None and lo == 0:
                        pe.wait_ge(bands_ready, tally(bands_ready))
                        pe.wait_ge(loaded_halo_w, tally(loaded_halo_w, 16 * 4))
                    if lo == 0:
                        pe.wait_ge(gray_ready, tally(gray_ready))
                        pe.wait_ge(halo_here, tally(halo_here, 16 * 6))
                    for k in range(lo, hi):
                        ps = take_bank(f"edges.{k}")
                        for t in range(TT):
                            for dx in range(3):
                                pe.matmul(ps[:, D * t:D * t + D], bands[:, k, dx, :], gray[:, t, dx:dx + D],
                                          start=(dx == 0), stop=False)
                            mm = pe.matmul(ps[:, D * t:D * t + D], halo_w[:, k, t, :], halo[:, t, :], start=False, stop=True)
                        mm.then_inc(pe_act[BANK[f"edges.{k}"]], 1)
                if step == "ffn_up":
                    if lo == 0:
                        copied("xn2_t")
                    features("ffn_up", w1_sb, xn2_t, lo, hi)
                if step == "xn_t":
                    pe.wait_ge(xn_ready, tally(xn_ready, 2))
                    transposes("xn_t", pe_act)
                if step == "ffn_down":
                    if lo == 0:
                        for u in range(WF // 2):
                            copied(f"ffn_up.{u}")
                        take_bank("ffn_down")
                    ps = bank("ffn_down")
                    for t in range(lo, hi):
                        for f in range(WF):
                            mm = pe.matmul(ps[:, D * t:D * t + D], wide[:, f, P * t:P * t + P], w2_sb[:, f, :],
                                           start=(f == 0), stop=(f == WF - 1))
                    if hi == TT:
                        mm.then_inc(pe_dve[BANK["ffn_down"]], 1)
                if step == "q":
                    if i is None and lo == 0:
                        pe.wait_ge(loaded_wq, tally(loaded_wq, 16))
                    if lo == 0:
                        copied("xn_t")
                    features("q", wq_sb, xn_t[:, :, MEM:J], lo, hi)
                if step == "k":
                    if i is None and lo == 0:
                        constants()
                        pe.wait_ge(loaded_wk, tally(loaded_wk, 16))
                    features("k", wk_sb, xn_t[:, :, MEM:J], lo, hi)
                if step in ("sum_q", "sum_k"):
                    sums_of_squares(step)
                if step in ("norms_q", "norms_k"):
                    src, name = (sums_q, "sum_q") if step == "norms_q" else (sums_k, "sum_k")
                    copied(name)
                    ps = take_bank(step)
                    for t in range(TT):
                        mm = pe.transpose(ps[:, P * t:P * t + P], src[:, P * t:P * t + P], ident[:])
                    mm.then_inc(pe_act[BANK[step]], 1)
                if step == "k_norms":
                    pe.wait_ge(k_root_ready, tally(k_root_ready))
                    ps = take_bank("k_norms")
                    for t in range(TT):
                        mm = pe.transpose(ps[:, P * t:P * t + P], norm_rows[:, t, :], ident[:])
                    mm.then_inc(pe_act[BANK["k_norms"]], 1)
                if step == "scale_k":
                    copied("k_norms")
                    for g in range(4):
                        ps = take_bank(f"scale_k.{g}")
                        rows = slice(32 * g, 32 * g + 32)
                        for e in range(2):
                            mm = pe.matmul(ps[:, N * e:N * e + N], head_back[rows, e, :], norm_cols[rows], start=True, stop=True)
                        mm.then_inc(pe_dve[BANK[f"scale_k.{g}"]], 1)
                if step == "dots0":
                    for u in range(lo, hi):
                        h = 4 * (u // 2) + u % 2
                        dots(f"dots0.{u}", 0, [h, h + 2], J0)

            run(pe, tally.settle, prologue, background, core, lambda: post_products(NP - 1))

        @block.scalar
        def _(act):
            tally = Tally(act)
            at = {}

            def full(u):
                act.wait_ge(pe_act[BANK[u]], tally(pe_act[BANK[u]]))
                return bank(u)

            def both(ins, u, ready):
                ins.then_inc(act_step, 1)
                act.wait_ge(act_step, tally(act_step))
                act.sem_inc(bank_free[BANK[u]], 1)
                act.sem_inc(ready, 1)

            def free(ins, u):
                ins.then_inc(bank_free[BANK[u]], 1)

            def halves(ps):
                return ps[:].rearrange("p (e n) -> p e n", e=2)

            def prologue():
                act.sem_inc(scores_free, 4)
                act.sem_inc(h_kept, 1)
                act.sem_inc(out_stored, 16)
                act.dma_start(x_in[:], x[0].rearrange("c (t p) d -> p c t d", p=P)).then_inc(x_here, 16)

            def constants():
                act.wait_ge(const_act, tally(const_act))
                ps = full("scale_k.0")
                for e in range(2):
                    rows = slice(DH * e, DH * e + DH)
                    src = ps[rows, 0:H * MEM].rearrange("p (f e m) -> p f e m", e=2, m=MEM)[:, :, e, :]
                    ins = act.copy(k_t[rows, :, 0:MEM], src)
                free(ins, "scale_k.0")
                free(act.copy(head_back[:], full("scale_k.1")[:, 0:2 * P].rearrange("p (f n) -> p f n", f=2)), "scale_k.1")

            def copy_scores(s):
                act.wait_ge(scores_free, tally(scores_free))
                r = s % 2
                act.wait_ge(score_full[r], tally(score_full[r]))
                for at, ks, n in score_parts(ORDER[s]):
                    ins = act.copy(scores[:, s % 4, ks[0]:ks[-1] + 1, 0:n],
                                   score_ps[r][:, at:at + len(ks) * n].rearrange("p (k n) -> p k n", n=n))
                ins.then_inc(act_step, 1)
                act.wait_ge(act_step, tally(act_step))
                act.sem_inc(score_free[r], 1)
                act.sem_inc(scores_copied, 1)
                act.sem_inc(by_row_free[r], 1)

            def exponentials(s):
                act.wait_ge(max_ready, tally(max_ready))
                for k in range(2):
                    b = 2 * ORDER[s] + k
                    n = cols(b)
                    kind = plan(b)[0]
                    act.activation(probs[:, s % 2, k, 0:n], scores[:, s % 4, k, 0:n], ACT.Exp,
                                   bias=neg_max[:, s % 2, k:k + 1], scale=-1.0 if kind == "low" else 1.0,
                                   accum_out=total[:, s % 2, k:k + 1] if kind == "all" else None).then_inc(exp_ready, 1)

            def normalise_mix(s):
                act.wait_ge(inv_ready, tally(inv_ready))
                for k in range(2):
                    act.mul(mix_n[:, s % 2, k, :], post_mix[:], inv_total[:, s % 2, k:k + 1]).then_inc(mix_ready, 1)

            def copy_probs(s):
                for k in range(2):
                    b = 2 * ORDER[s] + k
                    n = cols(b)
                    act.wait_ge(pt_full[k], tally(pt_full[k]))
                    for t, j0 in enumerate(range(0, n, P)):
                        m = min(P, n - j0)
                        src = pt_ps[k][0:m, P * t:P * t + P].rearrange("p (r h) -> p h r", h=H)
                        dst = (pt0[0:m, :, R * b:R * b + R], pt1[0:m, :, R * b - I1:R * b - I1 + R] if b >= NB // 2 - 1 else None,
                               pt_rest)[t]
                        ins = act.copy(dst, src)
                    ins.then_inc(pt_free[k], 1)

            def core(s, first, last):
                if s is None:
                    copy_scores(0)
                    copy_scores(1)
                    exponentials(0)
                    return
                if not (s == 0 and first):
                    copy_probs((s - 1) % NP)
                if s + 2 < NP or not last:
                    copy_scores((s + 2) % NP)
                at["slot"], at["more"] = s, s + 1 < NP or not last

            def normalise(w, src):
                act.wait_ge(rstd_ready, tally(rstd_ready))
                for t in range(TT):
                    act.activation(xn[:, t], src[:, t], ACT.Identity, bias=shift[:, w, t:t + 1], scale=rstd[:, w, t:t + 1]
                                   ).then_inc(xn_ready, 1)

            def background(step, i, lo=0, hi=1):
                if step == "load_x" and i is not None:
                    act.wait_ge(x_used, tally(x_used))
                    act.dma_start(x_in[:], x[i + 1].rearrange("c (t p) d -> p c t d", p=P)).then_inc(x_here, 16)
                if step == "softmax":
                    normalise_mix(at["slot"])
                    if at["more"]:
                        exponentials((at["slot"] + 1) % NP)
                if step in ("dots1", "dots0") and lo == 0:
                    act.wait_ge(q_root_ready, tally(q_root_ready))
                if step == "dots1":
                    for h in range(lo, hi):
                        u = f"dots1.{h}"
                        ps = full(u)
                        ins = act.mul(dots1[:, h, :], ps[:, 0:J], q_scale(1, h))
                        both(ins, u, dots_ready) if h == H - 1 else free(ins, u)
                if step == "dots0":
                    for n in range(lo, hi):
                        u = f"dots0.{n}"
                        ps = full(u)
                        h = 4 * (n // 2) + n % 2
                        for e in range(2):
                            ins = act.mul(dots0[:, h + 2 * e, :], ps[:, J0 * e:J0 * e + J0], q_scale(0, h + 2 * e))
                        both(ins, u, dots_ready) if n == 7 else free(ins, u)
                if step == "norms_q":
                    ps = full(step)
                    for t in range(TT):
                        ins = act.copy(qscale[:, t], ps[:, P * t:P * t + P].rearrange("p (g r) -> p g r", g=4)[:, :, 0:4])
                    both(ins, step, sums_ready)
                if step == "norms_k":
                    ps = full(step)
                    both(act.copy(norm_rows, ps[:, 0:TT * P].rearrange("p (t n) -> p t n", t=TT)), step, sums_ready)
                if step == "k_norms":
                    free(act.copy(norm_cols, full("k_norms")[:, 0:N]), "k_norms")
                if step == "v":
                    for n in range(lo, hi):
                        u = f"v.{n}"
                        ps = full(u)
                        jt, half = divmod(n, 2)
                        if n == 4:
                            for g in range(4):
                                ins = act.copy(v_rest[:, HD // 4 * g:HD // 4 * (g + 1)], ps[32 * g:32 * g + REST, 0:HD // 4])
                            free(ins, u)
                            continue
                        ins = act.copy(v_sb[:, jt, 512 * half:512 * half + 512], ps[:])
                        if n != 1:
                            free(ins, u)
                            continue
                        ins.then_inc(act_step, 1)
                        act.wait_ge(act_step, tally(act_step))
                        act.sem_inc(bank_free[BANK[u]], 1)
                        act.dma_start(v_sb[0:MEM, 0, :].rearrange("m (h d) -> m h d", h=H),
                                      mem_v.rearrange("h m d -> m h d")).then_inc(mem_v_here, 16)
                if step == "gate":
                    for n in range(lo, hi):
                        u = f"gate.{n}"
                        ps = full(u)
                        for e in range(2):
                            f = 2 * n + e
                            ins = act.activation(gate_t[:, f, :], ps[:, N * e:N * e + N], ACT.Tanh,
                                                 bias=half_bg[:, f:f + 1], scale=0.5)
                        both(ins, u, gates_ready) if n == FT // 2 - 1 else free(ins, u)
                if step == "norm2":
                    normalise(1, h_mid)
                if step == "xn2_t":
                    u = "xn2_t"
                    ps = full(u)
                    act.wait_ge(out_stored, tally(out_stored, 16))
                    both(act.copy(xn2_t[:], halves(ps)), u, xn2_done)
                if step == "edges":
                    if lo == 0:
                        act.wait_ge(h_kept, tally(h_kept))
                    for k, dst in ((0, h_new[:]), (1, abs_v))[lo:hi]:
                        u = f"edges.{k}"
                        ps = full(u)
                        ins = act.activation(dst, halves(ps), ACT.Abs, scale=0.5)
                        both(ins, u, abs_ready) if k == 1 else free(ins, u)
                if step == "ffn_up":
                    for n in range(lo, hi):
                        u = f"ffn_up.{n}"
                        ps = full(u)
                        for e in range(2):
                            f = 2 * n + e
                            ins = act.activation(wide[:, f, :], ps[:, N * e:N * e + N], ACT.Relu, bias=b1_sb[:, f:f + 1])
                        free(ins, u)
                if step == "norm1":
                    normalise(0, h_new)
                if step == "xn_t":
                    free(act.copy(xn_t[:, :, MEM:J], halves(full("xn_t"))), "xn_t")
                if step == "k" and i is None and lo == 0:
                    constants()
                if step in ("q", "k"):
                    dst = q_t if step == "q" else k_t[:, :, MEM:J]
                    for n in range(lo, hi):
                        u = f"{step}.{n}"
                        ps = full(u)
                        act.copy(dst[:, 2 * n:2 * n + 2], halves(ps))
                        free(act.activation(squares[step][:, 2 * n:2 * n + 2], halves(ps), ACT.Square), u)
                if step in ("sum_q", "sum_k"):
                    n = ("sum_q", "sum_k").index(step)
                    ps = full(step)
                    free(act.copy((sums_q, sums_k)[n], ps[:, 0:N]), step)

            run(act, tally.settle, prologue, background, core, lambda: copy_probs(NP - 1))
            act.wait_ge(out_stored, tally(out_stored, 16))

        @block.vector
        def _(dve):
            tally = Tally(dve)

            def full(u):
                dve.wait_ge(pe_dve[BANK[u]], tally(pe_dve[BANK[u]]))
                return bank(u)

            def prologue():
                dve.sem_inc(h_mid_free, 1)
                dve.wait_ge(loaded_filters, tally(loaded_filters, 16))
                dve.wait_ge(taps_ready, tally(taps_ready))
                for dy in range(3):
                    for k in range(2):
                        for dx in range(3):
                            tap = dots1[:, 3, 9 * k + 3 * dy + dx:9 * k + 3 * dy + dx + 1]
                            band = bands[:, k, dx, :]
                            if dy == 0:
                                ins = dve.tensor_scalar(band, dots1[:, dy, 0:P], tap, None, ALU.mult)
                            else:
                                ins = dve.scalar_tensor_tensor(out=band, in0=dots1[:, dy, 0:P], scalar=tap, in1=band,
                                                               op0=ALU.mult, op1=ALU.add)
                            ins.then_inc(dve_step, 1)
                    dve.wait_ge(dve_step, tally(dve_step, 6))
                dve.sem_inc(bands_ready, 1)

            def memory_norms():
                dve.wait_ge(const_dve, tally(const_dve))
                mem = slice(0, H * MEM)
                dve.scalar_tensor_tensor(out=dots0[mem, 1, 0:DH], in0=dots1[mem, 5, 0:DH], scalar=1.0,
                                         in1=dots1[mem, 5, 0:DH], op0=ALU.mult, op1=ALU.mult,
                                         accum_out=total[mem, 0, 0:1]).then_inc(mv_ready, 1)

            def views(s):
                p = ORDER[s]
                return ([plan(2 * p + k) for k in range(2)],
                        [scores[:, s % 4, k, 0:cols(2 * p + k)] for k in range(2)],
                        [work[:, k, 0:cols(2 * p + k)] for k in range(2)])

            def find_max(s):
                dve.wait_ge(scores_ready, tally(scores_ready, 2))
                for k, src in enumerate(views(s)[1]):
                    dve.max(top8[:, s % 2, k, :], src).then_inc(max_step[k], 1)

            def give_max(s):
                plans, src, _ = views(s)
                for k in range(2):
                    dve.wait_ge(max_step[k], tally(max_step[k]))
                    if plans[k][0] == "low":
                        dve.tensor_scalar(src[k], src[k], -1.0, None, ALU.mult).then_inc(max_step[k], 1)
                for k in range(2):
                    if plans[k][0] == "low":
                        dve.wait_ge(max_step[k], tally(max_step[k]))
                dve.tensor_scalar(neg_max[:, s % 2, :], top8[:, s % 2, :, 0], -1.0, None, ALU.mult).then_inc(max_ready, 1)

            def start_cut(s):
                plans, src, wrk = views(s)
                for k in range(2):
                    if plans[k][0] == "low":
                        dve.max(cut8[:, k, :], src[k]).then_inc(block_step[k], 1)
                    elif plans[k][0] == "top":
                        dve.match_replace(wrk[k], top8[:, s % 2, k, :], src[k], TAKEN).then_inc(block_step[k], 1)

            def find_cut(s):
                plans, src, wrk = views(s)
                for r in range(1, 8):
                    for k in range(2):
                        if r < plans[k][1] and not (r == 1 and plans[k][0] == "top"):
                            dve.wait_ge(block_step[k], tally(block_step[k]))
                            dve.match_replace(wrk[k], cut8[:, k, :], src[k] if r == 1 else wrk[k], TAKEN
                                              ).then_inc(block_step[k], 1)
                    for k in range(2):
                        if r < plans[k][1]:
                            dve.wait_ge(block_step[k], tally(block_step[k]))
                            dve.max(cut8[:, k, :], wrk[k]).then_inc(block_step[k], 1)

            def cut_and_sum(s):
                p = ORDER[s]
                dve.wait_ge(exp_ready, tally(exp_ready, 2))
                for k in range(2):
                    kind, rounds, at = plan(2 * p + k)
                    n = cols(2 * p + k)
                    if kind == "all":
                        continue
                    dve.wait_ge(block_step[k], tally(block_step[k]))
                    pr = probs[:, s % 2, k, 0:n]
                    dve.scalar_tensor_tensor(out=pr, in0=scores[:, s % 4, k, 0:n], scalar=cut8[:, k, at:at + 1], in1=pr,
                                             op0=ALU.is_ge if kind == "top" else ALU.is_le, op1=ALU.mult,
                                             accum_out=total[:, s % 2, k:k + 1]).then_inc(sum_step, 1)

            def give_inverse(s):
                summed = [k for k in range(2) if plan(2 * ORDER[s] + k)[0] != "all"]
                if summed:
                    dve.wait_ge(sum_step, tally(sum_step, len(summed)))
                dve.reciprocal(inv_total[:, s % 2, :], total[:, s % 2, :]).then_inc(inv_ready, 1)
                dve.sem_inc(scores_free, 1)

            def core(s, first, last):
                more = s is None or s + 1 < NP or not last
                new = 0 if s is None else (s + 1) % NP
                if more:
                    find_max(new)
                if s is not None:
                    cut_and_sum(s)
                if more:
                    give_max(new)
                    start_cut(new)
                if s is not None:
                    give_inverse(s)
                if more:
                    find_cut(new)

            def moments(w, src):
                for t in range(TT):
                    dve.bn_stats(stats[:, t, :], src[:, t]).then_inc(dve_step, 1)
                for t in range(TT):
                    dve.wait_ge(dve_step, tally(dve_step))
                    dve.bn_aggr(mv[:, w, t, :], stats[:, t, :]).then_inc(mv_ready, 1)

            def gate_heads():
                for g in range(FT // 2):
                    u = f"values.{g}"
                    ps = full(u)
                    fs = slice(2 * g, 2 * g + 2)
                    if g == 0:
                        dve.wait_ge(gates_ready, tally(gates_ready))
                    dve.scalar_tensor_tensor(out=heads_t[:, fs, :], in0=gate_t[:, fs, :], scalar=1.0,
                                             in1=ps[:].rearrange("p (f n) -> p f n", n=N), op0=ALU.add, op1=ALU.mult
                                             ).then_inc(bank_free[BANK[u]], 1)

            def background(step, i, lo=0, hi=1):
                if step == "gate_heads":
                    gate_heads()
                if step == "add_project":
                    ps = full("project")
                    dve.wait_ge(h_moved, tally(h_moved))
                    dve.tensor_tensor(h_mid[:], h_mid[:], ps[:].rearrange("p (t d) -> p t d", t=TT), ALU.add).then_inc(dve_step, 1)
                    dve.wait_ge(dve_step, tally(dve_step))
                    dve.sem_inc(bank_free[BANK["project"]], 1)
                    moments(1, h_mid)
                if step == "moments":
                    dve.wait_ge(h_ready, tally(h_ready))
                    moments(0, h_new)
                    if i is None:
                        memory_norms()
                if step == "add_output":
                    u = "ffn_down"
                    ps = full(u)
                    dve.wait_ge(h_mid_ready, tally(h_mid_ready))
                    dve.tensor_tensor(out_sb[:], h_mid[:], ps[:].rearrange("p (t d) -> p t d", t=TT), ALU.add
                                      ).then_inc(dve_step, 1)
                    dve.wait_ge(dve_step, tally(dve_step))
                    dve.sem_inc(bank_free[BANK[u]], 1)
                    dve.sem_inc(out_ready, 1)
                    dve.sem_inc(h_mid_free, 1)
                if step == "scale_k":
                    for n in range(FT // 2):
                        u = f"scale_k.{n}"
                        ps = full(u)
                        keys = k_t[:, n:n + 5:4, MEM:J]
                        dve.tensor_tensor(keys, keys,
                                          ps[:].rearrange("p (e n) -> p e n", e=2), ALU.mult).then_inc(bank_free[BANK[u]], 1)

            run(dve, tally.settle, prologue, background, core)


_INS = ["x", "L0_tok_scharr", "L0_attn_Wq", "L0_attn_Wk", "L0_attn_Wv", "L0_attn_W_pre_th", "L0_attn_W_post_th", "L0_attn_mem_k",
        "L0_attn_mem_v", "L0_attn_head_scale_params", "L0_attn_Wg", "L0_attn_bg", "L0_attn_Wo", "L0_ffn_w1", "L0_ffn_b1",
        "L0_ffn_w2", "L0_ffn_b2"]


def kernel(**inputs):
    import numpy as _np
    import concourse.bacc as _bacc
    from concourse import mybir as _mybir
    from concourse.bass_utils import run_bass_kernel_spmd as _run

    nc = _bacc.Bacc("TRN2", target_bir_lowering=False, num_devices=1)
    arrays, args = {}, []
    for name in _INS:
        a = _np.ascontiguousarray(inputs[name])
        arrays[f"in_{name}_dram"] = a
        args.append(nc.dram_tensor(f"in_{name}_dram", a.shape, _mybir.dt.from_np(a.dtype), kind="ExternalInput").ap())
    n, _, rows, width = inputs["x"].shape
    out = nc.dram_tensor("out_dram", (n, rows, width), _mybir.dt.float32, kind="ExternalOutput").ap()
    vit_layer(nc, *args, out)
    r = _run(nc, [arrays], core_ids=[0])
    return r.results[0]["out_dram"]
```
